# Optimizing a Trainium2 kernel written in Bass

```python
import numpy as np
import jax
import jax.numpy as jnp

def _softmax(x, axis=-1):
    return jax.nn.softmax(x, axis=axis)

def _gelu(x):
    return jax.nn.gelu(x, approximate=True)

def _silu(x):
    return jax.nn.silu(x)

def _sigmoid(x):
    return jax.nn.sigmoid(x)

def _layernorm(x, axis=-1, eps=1e-05):
    m = jnp.mean(x, axis=axis, keepdims=True)
    v = jnp.var(x, axis=axis, keepdims=True)
    return (x - m) / jnp.sqrt(v + eps)

def _scatter_add(tgt, idx, src, axis=0):
    return tgt.at[idx].add(src)

def _segment_sum(src, seg, n):
    return jax.ops.segment_sum(src, seg, n)
kernel_name = 'mk_adaln_d1_jaxref_r8_e04ca5'

def setup_inputs(seed: int=0):
    np.random.seed(seed)
    _w = jnp.asarray

    def _L0_attn_setup():
        import jax, jax.numpy as jnp
        import numpy as np
        DIM = 256
        HEADS = 32
        WINDOW = 8
        B = 4
        N = 197

        def _local_mask(w, n):
            i = jnp.arange(n)[:, None]
            j = jnp.arange(n)[None, :]
            d = jnp.abs(i - j).astype(jnp.float32)
            in_win = (j >= i - w) & (j < i + w)
            return jnp.where(in_win, (w - d / 2.0) / w, 0.0)
        key = jax.random.key(seed)
        k1, k2, k3, k4 = jax.random.split(key, 4)
        x = jax.random.normal(k1, (B, N, DIM), dtype=jnp.float32)
        qkv_w = jax.random.normal(k2, (3 * DIM, DIM), dtype=jnp.float32) * 0.02
        proj_w = jax.random.normal(k3, (DIM, DIM), dtype=jnp.float32) * 0.02
        proj_b = jax.random.normal(k4, (DIM,), dtype=jnp.float32) * 0.02
        return {'x': x, 'qkv_w': qkv_w, 'proj_w': proj_w, 'proj_b': proj_b}
    _L0_attn_in = _L0_attn_setup()

    def _L0_ffn_setup():
        import jax, jax.numpy as jnp
        import numpy as np
        TOPK = 2

        def _mlp(x, w1, w2, w3):
            a = jnp.dot(x, w1.T).astype(jnp.float32)
            b = jnp.dot(x, w3.T).astype(jnp.float32)
            h = (jax.nn.silu(a) * b).astype(x.dtype)
            return jnp.dot(h, w2.T)
        key = jax.random.key(seed)
        ks = jax.random.split(key, 8)
        B, S, D, I, E = (4, 256, 256, 176, 16)
        SI = I * 2
        sc = 0.02
        return {'x': jax.random.normal(ks[0], (B, S, D), jnp.bfloat16), 'gate_w': jax.random.normal(ks[1], (E, D), jnp.float32) * sc, 'w1': jax.random.normal(ks[2], (E, I, D), jnp.bfloat16) * sc, 'w2': jax.random.normal(ks[3], (E, D, I), jnp.bfloat16) * sc, 'w3': jax.random.normal(ks[4], (E, I, D), jnp.bfloat16) * sc, 'sw1': jax.random.normal(ks[5], (SI, D), jnp.bfloat16) * sc, 'sw2': jax.random.normal(ks[6], (D, SI), jnp.bfloat16) * sc, 'sw3': jax.random.normal(ks[7], (SI, D), jnp.bfloat16) * sc}
    _L0_ffn_in = _L0_ffn_setup()
    _L0_c = _w((lambda *s: np.random.randn(*s).astype(np.float32) * 0.05)(8, 256))
    _L0_wmod = _w((lambda *s: np.random.randn(*s).astype(np.float32) * 0.05)(256, 6 * 256) * 256 ** (-0.5))
    _d = {'L0_attn_x': _L0_attn_in['x'], 'L0_attn_qkv_w': _L0_attn_in['qkv_w'], 'L0_attn_proj_w': _L0_attn_in['proj_w'], 'L0_attn_proj_b': _L0_attn_in['proj_b'], 'L0_ffn_gate_w': _L0_ffn_in['gate_w'], 'L0_ffn_w1': _L0_ffn_in['w1'], 'L0_ffn_w2': _L0_ffn_in['w2'], 'L0_ffn_w3': _L0_ffn_in['w3'], 'L0_ffn_sw1': _L0_ffn_in['sw1'], 'L0_ffn_sw2': _L0_ffn_in['sw2'], 'L0_ffn_sw3': _L0_ffn_in['sw3'], 'L0_c': _L0_c, 'L0_wmod': _L0_wmod}
    _x0 = _d['L0_attn_x']
    _d['L0_attn_x'] = jax.random.normal(jax.random.fold_in(jax.random.key(seed), 1), (8, 256, 256), dtype=_x0.dtype)
    del _x0
    return _d

def reference(L0_attn_x, L0_attn_qkv_w, L0_attn_proj_w, L0_attn_proj_b, L0_ffn_gate_w, L0_ffn_w1, L0_ffn_w2, L0_ffn_w3, L0_ffn_sw1, L0_ffn_sw2, L0_ffn_sw3, L0_c, L0_wmod):

    def _L0_attn_ref(x, qkv_w, proj_w, proj_b):
        import jax, jax.numpy as jnp
        import numpy as np
        DIM = 256
        HEADS = 32
        WINDOW = 8
        B = 4
        N = 197

        def _local_mask(w, n):
            i = jnp.arange(n)[:, None]
            j = jnp.arange(n)[None, :]
            d = jnp.abs(i - j).astype(jnp.float32)
            in_win = (j >= i - w) & (j < i + w)
            return jnp.where(in_win, (w - d / 2.0) / w, 0.0)
        Bb, Nn, C = x.shape
        H = HEADS
        hd = C // H
        scale = hd ** (-0.5)
        qkv = (x @ qkv_w.T).reshape(Bb, Nn, 3, H, hd).transpose(2, 0, 3, 1, 4)
        q, k, v = (qkv[0], qkv[1], qkv[2])
        attn = jnp.einsum('bhnd,bhmd->bhnm', q, k) * scale
        m = _local_mask(WINDOW, Nn)
        attn = jnp.where(m != 0.0, attn * m, -jnp.inf)
        attn = jax.nn.softmax(attn, axis=-1)
        out = jnp.einsum('bhnm,bhmd->bhnd', attn, v)
        out = out.transpose(0, 2, 1, 3).reshape(Bb, Nn, C)
        return out @ proj_w.T + proj_b

    def _L0_ffn_ref(x, gate_w, w1, w2, w3, sw1, sw2, sw3):
        import jax, jax.numpy as jnp
        import numpy as np
        TOPK = 2

        def _mlp(x, w1, w2, w3):
            a = jnp.dot(x, w1.T).astype(jnp.float32)
            b = jnp.dot(x, w3.T).astype(jnp.float32)
            h = (jax.nn.silu(a) * b).astype(x.dtype)
            return jnp.dot(h, w2.T)
        B, S, D = x.shape
        E = gate_w.shape[0]
        xf = x.reshape(-1, D)
        T = xf.shape[0]
        scores = jax.nn.sigmoid(jnp.dot(xf.astype(jnp.float32), gate_w.T))
        topv, topi = jax.lax.top_k(scores, TOPK)
        topv = topv / topv.sum(axis=-1, keepdims=True)
        dw = jnp.zeros((T, E), jnp.float32).at[jnp.arange(T)[:, None], topi].add(topv)
        y0 = _mlp(xf, sw1, sw2, sw3).astype(jnp.float32)

        def step(y, ws):
            e1, e2, e3, we = ws
            out = _mlp(xf, e1, e2, e3).astype(jnp.float32)
            return (y + out * we[:, None], None)
        y, _ = jax.lax.scan(step, y0, (w1, w2, w3, dw.T))
        return y.astype(x.dtype).reshape(B, S, D)
    x = L0_attn_x
    mod = (_silu(L0_c) @ L0_wmod).reshape(L0_c.shape[0], 6, 1, -1)
    sa, ca, ga, sb, cb, gb = (mod[:, 0], mod[:, 1], mod[:, 2], mod[:, 3], mod[:, 4], mod[:, 5])
    ga = (2 * (ga >= 0) - 1) * jnp.maximum(jnp.abs(ga), 0.25)
    gb = (2 * (gb >= 0) - 1) * jnp.maximum(jnp.abs(gb), 0.25)
    h = _layernorm(x, axis=-1) * (1 + ca) + sa
    x = x + ga * _L0_attn_ref(h, L0_attn_qkv_w, L0_attn_proj_w, L0_attn_proj_b)
    h = _layernorm(x, axis=-1) * (1 + cb) + sb
    x = x + gb * _L0_ffn_ref(h, L0_ffn_gate_w, L0_ffn_w1, L0_ffn_w2, L0_ffn_w3, L0_ffn_sw1, L0_ffn_sw2, L0_ffn_sw3)
    return x

_drawn_inputs = setup_inputs


def setup_inputs(seed=0):
    import zlib

    import numpy as np

    out = dict(_drawn_inputs(seed))
    spreads = {}
    factors = {'L0_attn_qkv_w': 8.0,
     'L0_attn_proj_w': 8.0,
     'L0_attn_proj_b': 8.0,
     'L0_ffn_gate_w': 8.0,
     'L0_ffn_w1': 8.0,
     'L0_ffn_w2': 8.0,
     'L0_ffn_w3': 8.0,
     'L0_ffn_sw1': 8.0,
     'L0_ffn_sw2': 8.0,
     'L0_ffn_sw3': 8.0,
     'L0_c': 5.675,
     'L0_wmod': 5.654}
    for name, (base, spread) in spreads.items():
        noise = np.random.default_rng([zlib.crc32(name.encode()), seed]).standard_normal(out[name].shape)
        drawn = base * np.exp(spread * noise) if base else spread * noise
        out[name] = jnp.asarray(drawn.astype(out[name].dtype))
    for name, factor in factors.items():
        out[name] = (out[name] * factor).astype(out[name].dtype)
    return out
```

```python
from contextlib import ExitStack

import concourse.bass as bass
import numpy as np
from concourse import mybir

F32 = mybir.dt.float32
I32 = mybir.dt.int32
BF16 = mybir.dt.bfloat16
ALU = mybir.AluOpType
ACT = mybir.ActivationFunctionType
AX = mybir.AxisListType

B, N, D = 8, 256, 256
T = B * N
P = 128
C = D // P
TT = T // P
U = N // P
HEADS, HD, WIN = 32, 8, 8

QB = 16
KB = 2 * QB
GH = P // QB
GC = GH * HD
G = D // GC
BL = P // QB
NBLK = G * BL
BPT = P // KB
PADN = WIN + N + WIN
EPS = 1e-5

E, I, SI, TOPK = 16, 176, 352, 2
IH = I // 2
SK = -(-SI // P)
PARTS = 3
NS = T * TOPK // P + E
RING = 4
AHEAD = 3
SHARED_W = (P, SK)
EXPERT_W = (IH, 2)
NONE = 8192

FC = {}
_w = 0
for _n, _k in (("ident", P), ("window", P), ("headsel", GH), ("nhalf", 2), ("rev", E), ("lane", P), ("tile", NS),
               ("turn", TOPK * TT), ("row1", 1), ("one", E)):
    FC[_n] = (_w, _w + _k)
    _w += _k
FCW = _w
BCW = P + 2 * 4 * P + 2 * P


def build(nc, x, wqkvT, projT, proj_b, cT, wmod, gateT, w13T, w2T, sw13T, sw2T, cf, cb, out):
    ctx = ExitStack()
    with ctx:
        def sb(name, shape, dt=F32):
            return ctx.enter_context(nc.sbuf_tensor(name, shape, dt))

        def sem(name):
            return ctx.enter_context(nc.semaphore(name))

        class Region:

            def __init__(self, tensor):
                self.tensor, self.at = tensor, 0

            def take(self, pattern, shape, dt=F32):
                n = int(np.prod([v for v in shape])) * (2 if dt == BF16 else 4) // 4
                v = self.tensor[:, self.at:self.at + n]
                self.at += n
                assert self.at <= self.tensor.shape[1]
                if dt != F32:
                    v = v.bitcast(dt)
                if len(shape) == 1:
                    return v
                names = pattern.split()
                return v.rearrange(f"p ({pattern}) -> p {pattern}", **dict(zip(names[1:], shape[1:])))

        first_region = sb("first_region", [P, C * 6 * D])
        setup = Region(first_region)
        picks = Region(first_region)
        second_region = sb("second_region", [P, 6720])
        attn = Region(second_region)
        late = Region(second_region)
        xs = sb("xs", [P, TT, D])
        cft = sb("cft", [P, FCW])
        cbt = sb("cbt", [P, BCW], BF16)
        wqkv = attn.take("c n", (C, 3 * D,))
        wpj = attn.take("c n", (C, D,))
        pb = sb("pb", [1, D])
        ones_row = sb("ones_row", [1, P])
        cts = sb("cts", [P, C, B])
        csig = sb("csig", [P, C, B])
        wms = setup.take("c n", (C, 6 * D,))
        modrow = sb("modrow", [B, 6 * D])
        gtmp = sb("gtmp", [B, 4, D])
        modT = sb("modT", [P, 4, B])
        modb = sb("modb", [P, B, 4 * D])

        bst2 = sb("bst2", [P, U, 6])
        mv2 = sb("mv2", [P, U, 2])
        ve2 = sb("ve2", [P, U])
        rstd2s = sb("rstd2s", [P, U])
        bst = sb("bst", [P, U, 6])
        mv = sb("mv", [P, U, 2])
        ve = sb("ve", [P, U])
        rstd = sb("rstd", [P, U])
        xn = attn.take("u d", (U, D,))
        hT = attn.take("c n", (C, PADN,))
        hw = attn.take("c b j", (C, N // QB, KB,))
        region = sb("region", [P, C * N * GH + 4 * 2048])
        at = C * N * GH
        qbd = region[:, 0:at].rearrange("p (c n h) -> p c n h", c=C, h=GH)
        kT = attn.take("c n", (C, PADN,))
        vw = attn.take("w d", (N // (QB * BPT), D,))
        ST = region[:, at:at + 2048].rearrange("p (u k j) -> p u k j", u=U, j=P)
        S = region[:, at + 2048:at + 4096].rearrange("p (u k j) -> p u k j", u=U, j=KB)
        mx = sb("mx", [P, U, NBLK])
        rs = sb("rs", [P, U, NBLK])
        ri = sb("ri", [P, U, NBLK])
        PT = region[:, at + 4096:at + 6144].rearrange("p (u k j) -> p u k j", u=U, j=P)
        Z = region[:, at + 6144:at + 8192].rearrange("p (z k h) -> p z k h", z=2, h=GH)
        w13n, w2n = C * E * SI // 2, 2 * E * D // 2
        w13 = region[:, 0:w13n].bitcast(BF16).rearrange("p (c e i) -> p c e i", c=C, e=E)
        w2 = region[0:IH, w13n:w13n + w2n].bitcast(BF16).rearrange("p (k e d) -> p k e d", k=2, e=E)
        yk = region[:, 0:TOPK * TT * D].rearrange("p (k t d) -> p k t d", k=TOPK, t=TT)
        OT = attn.take("u c t", (U, C, P,))
        ao = attn.take("u d", (U, D,))

        h2 = sb("h2", [P, U, D])
        hr = sb("hr", [P, U, D])
        h3 = sb("h3", [P, U, PARTS, D], BF16)
        xT = sb("xT", [P, TT, PARTS * C, P], BF16)
        gws = sb("gws", [P, C, E])
        gwr = sb("gwr", [P, C, E])
        gw3 = sb("gw3", [P, C, PARTS, E], BF16)
        sw13 = sb("sw13", [P, C, 2 * SI], BF16)
        sw2 = sb("sw2", [P, SK, D], BF16)
        logit = sb("logit", [P, TT, E])
        score = sb("score", [P, TT, E])
        cand = sb("cand", [P, TT, E])
        oh = sb("oh", [P, TOPK, TT, E])
        ohb = sb("ohb", [P, TT + 1, E], BF16)
        top = sb("top", [P, TOPK, TT])
        rtop = sb("rtop", [P, TOPK, TT])
        gatew = sb("gatew", [P, TOPK, TT])
        den = sb("den", [P, TT])
        cnt = sb("cnt", [P, 4, E])
        cnti = sb("cnti", [P, E], I32)
        pos = sb("pos", [P, TOPK * TT])
        posi = sb("posi", [P, 3, TOPK * TT], I32)
        posf = sb("posf", [P, 2, TOPK * TT])
        lane_oh = picks.take("k l", (TOPK * TT, P,), BF16)
        tile_oh = picks.take("k s", (TOPK * TT, NS,), BF16)
        val = late.take("k v s", (TOPK * TT, 2, NS,), BF16)
        owner = late.take("s e", (NS, E,))
        slot = sb("slot", [P, 4, NS])
        sloti = sb("sloti", [P, 2, NS], I32)
        expert = sb("expert", [P, NS], I32)
        ixg = sb("ixg", [P, RING], I32)
        ixp = sb("ixp", [P, RING], I32)
        rows = late.take("j n", (RING, PARTS * D,), BF16)
        rT = late.take("j q t", (2, PARTS * C, P,), BF16)
        act_s = late.take("j w", (2, SI,))
        hid = sb("hid", [P, 2, SK * P])
        hres = late.take("j k t", (2, SK, P,))
        hT3 = sb("hT3", [P, 2, PARTS, SK, P], BF16)
        yo = sb("yo", [P, RING, D])

        ident = cft[:, FC["ident"][0]:FC["ident"][1]]
        window = cft[:, FC["window"][0]:FC["window"][1]]
        headsel = cft[:, FC["headsel"][0]:FC["headsel"][1]]
        nhalf = cft[:, FC["nhalf"][0]:FC["nhalf"][1]]
        rev, lane, tileno, turn, row1, one = (cft[:, FC[n][0]:FC[n][1]] for n in (
            "rev", "lane", "tile", "turn", "row1", "one"))
        identb = cbt[:, 0:P]
        before = cbt[:, BCW - 2 * P:BCW - P]
        onesb = cbt[:, BCW - P:BCW]

        def addmask(u):
            return cbt[:, P + u * 4 * P:P + (u + 1) * 4 * P]

        bank = [ctx.enter_context(nc.psum_tensor(f"bank{i}", [P, 1024], F32)) for i in range(4)]
        SP = [bank[0], bank[1]]
        ZP = bank[2]
        M0 = bank[3][:, 0:512]
        M1 = bank[3][:, 512:1024]

        MB = [M0[:, 0:PARTS * D // 2].bitcast(BF16), M1[:, 0:PARTS * D // 2].bitcast(BF16)]
        LG = [m[:, PARTS * D // 2:PARTS * D // 2 + PARTS * E] for m in (M0, M1)]

        def HT(j):
            return bank[2][:, (j % 2) * 512:(j % 2) * 512 + SK * P].rearrange("p (k t) -> p k t", t=P)

        def YP(j):
            return bank[3][:, (j % 2) * 512:(j % 2) * 512 + D]

        def RTP(j):
            return bank[j % 2][:, 512:512 + PARTS * D // 2].bitcast(BF16)

        moddram = nc.dram_tensor("moddram", [B, 6 * D], F32, kind="Internal").ap()

        hrows = nc.dram_tensor("hrows", [T, PARTS * D], BF16, kind="Internal").ap()
        yrows = nc.dram_tensor("yrows", [TOPK * T, D], F32, kind="Internal").ap()

        l2_st, l2_mv, l2_ve, l2_rs, l2_xn, l2_mu, l2_h = (sem("l2_" + n) for n in (
            "st", "mv", "ve", "rs", "xn", "mu", "h"))
        p_hi, p_r, p_mid, p_lo, xT_p, xT_s, lg_p, lg_s, st_h = (sem(n) for n in (
            "p_hi", "p_r", "p_mid", "p_lo", "xT_p", "xT_s", "lg_p", "lg_s", "st_h"))
        ld_g, ld_sw, ld_ew, gw_s = (sem(n) for n in ("ld_g", "ld_sw", "ld_ew", "gw_s"))
        r_exp, rt, rank_p, slot_p, routed, ohb_s = (sem(n) for n in (
            "r_exp", "rt", "rank_p", "slot_p", "routed", "ohb_s"))
        val_s, passed = sem("val_s"), sem("passed")
        up_p, silu_s, hid_s, ht_p, hi_s, res_s, mid_s, lo_s, y_p, y_s = (sem("m_" + n) for n in (
            "up", "silu", "hid", "ht", "hi", "res", "mid", "lo", "y", "ys"))
        sh_s = sem("sh_s")
        ixg_s, ixp_s, rT_p, rT_s, yo_s = (sem(n) for n in ("ixg_s", "ixp_s", "rT_p", "rT_s", "yo_s"))
        fetch = [sem(f"fetch{k}") for k in range(RING)]
        put = [sem(f"put{k}") for k in range(RING)]
        ld_y = [sem(f"ld_y{k}") for k in range(B)]
        f_a, f_b, f_c, f_d = (sem("f_" + n) for n in "abcd")

        ld_cst, ld_x0, ld_x1, ld_w, ld_mod = (sem("ld_" + n) for n in ("cst", "x0", "x1", "w", "mod"))
        c_exp, c_den, c_inv, c_silu = (sem("c_" + n) for n in ("exp", "den", "inv", "silu"))
        mod_p, mod_r, g_sgn, g_abs, g_fin, modT_p, modT_s, mod_st, mod_ld = (sem(n) for n in (
            "mod_p", "mod_r", "g_sgn", "g_abs", "g_fin", "modT_p", "modT_s", "mod_st", "mod_ld"))
        pads, hw_s = sem("pads"), sem("hw_s")
        ln_st, ln_mv, ln_ve, ln_rs, ln_xn = (sem("ln_" + n) for n in ("st", "mv", "ve", "rs", "xn"))
        hT_p, hT_s, q_p, q_s, k_p, k_s, v_p, v_s = (sem(n) for n in (
            "hT_p", "hT_s", "q_p", "q_s", "k_p", "k_s", "v_p", "v_s"))
        s_p, s_m, st_p, s_mx, s_sub, s_ex, s_sum, s_ri, s_nm = (sem("s_" + n) for n in (
            "p", "m", "t", "mx", "sub", "ex", "sum", "ri", "nm"))
        pt_p, pt_s, z_p, z_s, o_s, pr_p, ga_s, x1_s = (sem(n) for n in (
            "pt_p", "pt_s", "z_p", "z_s", "o_s", "pr_p", "ga_s", "x1_s"))
        st_out = sem("st_out")

        block = ctx.enter_context(nc.Block())

        def wait(eng, s, v):
            if not (isinstance(v, int) and v <= 0):
                eng.wait_ge(s, v)

        def settle(eng):
            eng.sem_inc(passed, 1)

        def over(eng, main):
            main(0, True, False)
            with eng.Fori(1, B - 1) as it:
                main(it, False, False)
            main(B - 1, False, True)

        def over_tiles(eng, step, n, k):
            for j in range(k):
                step(j, j, 0)
            with eng.Fori(1, n // k - 1) as i:
                for j in range(k):
                    step(k * i + j, j, i)
            for j in range(k):
                step(n - k + j, j, n // k - 1)

        def later(i, j, d):
            q, r = divmod(j + d, RING)
            return RING * (i + q) + r, r, i + q

        x_t = x.rearrange("(t p) d -> p t d", p=P)

        @block.sync
        def _(sp):
            sp.dma_start(xs[:, 0:U, :], x_t[:, 0:U, :]).then_inc(ld_x0, 16)
            sp.dma_start(cts[:, :, :], cT.rearrange("(c p) b -> p c b", p=P)).then_inc(ld_cst, 16)
            sp.dma_start(wms[:, :, :], wmod.rearrange("(c p) n -> p c n", p=P)).then_inc(ld_cst, 16)
            sp.dma_start(xs[:, U:TT, :], x_t[:, U:TT, :]).then_inc(ld_x1, 16)
            sp.wait_ge(g_fin, 1)
            sp.dma_start(moddram, modrow[:, :]).then_inc(mod_st, 16)
            sp.wait_ge(mod_st, 16)
            sp.dma_start(modb[:, :, :], moddram[:, 2 * D:6 * D].partition_broadcast(P)).then_inc(mod_ld, 16)
            hrows_t = hrows.rearrange("(b u p) k -> b p u k", u=U, p=P)
            def store_h(b):
                wait(sp, p_lo, b + 1)
                sp.dma_start(hrows_t[b], h3[:, :, :, :].rearrange("p u k d -> p u (k d)")).then_inc(st_h, 16)
            store_h(0)
            with sp.Fori(1, B) as b:
                store_h(b)
            sp.wait_ge(x1_s, TT)
            sp.dma_start(w13, w13T).then_inc(ld_ew, 16)
            sp.dma_start(w2, w2T).then_inc(ld_ew, 16)
            y_t = yrows.rearrange("(k b u p) d -> b p k u d", k=TOPK, u=U, p=P)
            sp.wait_ge(y_p, TT + NS)
            for k in range(RING):
                sp.wait_ge(put[k], 16 * (NS // RING))
            for b in range(B):
                for k in range(TOPK):
                    sp.dma_start(yk[:, k, U * b:U * b + U, :], y_t[b, :, k]).then_inc(ld_y[b], 16)
            out_t = out.rearrange("(b u p) d -> b p u d", u=U, p=P)
            for b in range(B):
                sp.wait_ge(f_d, b + 1)
                sp.dma_start(out_t[b], xs[:, U * b:U * b + U, :]).then_inc(st_out, 16)
            sp.wait_ge(st_out, 16 * B)

        @block.gpsimd
        def _(gp):
            gp.memset(ones_row[:, :], 1.0)
            gp.memset(ohb[:, TT, :], 0.0)
            gp.memset(hid[:, :, :], 0.0)
            gp.memset(hT[:, :, :], 0.0)
            gp.memset(kT[:, :, :], 0.0).then_inc(pads, 1)
            gp.wait_ge(ld_w, 80)

            def rstd1(b):
                wait(gp, ln_ve, b + 1)
                gp.tensor_tensor(rstd[:, :], ve[:, :], nhalf, ALU.pow).then_inc(ln_rs, 1)

            def key_windows(b):
                wait(gp, hT_s, b + 1)
                wait(gp, v_p, b)
                settle(gp)
                for c in range(C):
                    a = hT[:, c, :]
                    last = gp.tensor_copy(hw[:, c], bass.AP(a.tensor, a.offset, [a.ap[0], [QB, N // QB], [1, KB]]))
                last.then_inc(hw_s, 1)

            def rstd2(b):
                wait(gp, l2_ve, b + 1)
                gp.tensor_tensor(rstd2s[:, :], ve2[:, :], nhalf, ALU.pow).then_inc(l2_rs, 1)

            def split(b):
                wait(gp, l2_xn, b + 1)
                gp.tensor_tensor(h2[:, :, :], h2[:, :, :],
                                 modb[:, b, 2 * D:3 * D].unsqueeze(1).to_broadcast([P, U, D]), ALU.mult).then_inc(l2_mu, 1)
                wait(gp, l2_mu, b + 1)
                gp.tensor_tensor(h2[:, :, :], h2[:, :, :],
                                 modb[:, b, D:2 * D].unsqueeze(1).to_broadcast([P, U, D]), ALU.add).then_inc(l2_h, 1)
                wait(gp, p_hi, b + 1)
                gp.tensor_tensor(hr[:, :, :], h2[:, :, :], h3[:, :, 0], ALU.subtract).then_inc(p_r, 1)
                wait(gp, p_mid, b + 1)
                gp.tensor_tensor(h3[:, :, 2], hr[:, :, :], h3[:, :, 1], ALU.subtract).then_inc(p_lo, 1)

            def main(it, first, final):
                if first:
                    gp.wait_ge(mod_ld, 16)
                else:
                    split(it - 1)
                if not final:
                    rstd1(it + 1)
                for u in range(U):
                    n = U * it + u
                    wait(gp, s_ri, n + 1)
                    gp.tensor_tensor(S[:, u], S[:, u], ri[:, u, :].unsqueeze(2).to_broadcast([P, NBLK, KB]),
                                     ALU.mult).then_inc(s_nm, 1)
                if not final:
                    key_windows(it + 1)
                rstd2(it)

            rstd1(0)
            key_windows(0)
            over(gp, main)
            split(B - 1)

            def lo(n, w, j):
                p, k = w
                wait(gp, mid_s, n + 1)
                wait(gp, y_p, n - 1)
                gp.tensor_tensor(hT3[0:p, j % 2, 2, 0:k], hres[0:p, j % 2, 0:k], hT3[0:p, j % 2, 1, 0:k],
                                 ALU.subtract).then_inc(lo_s, 1)

            over_tiles(gp, lambda t, j, i: lo(t, SHARED_W, j), TT, 2)

            gp.wait_ge(st_h, 16 * B)
            gp.wait_ge(routed, 1)

            def get(s, j, i):
                wait(gp, rT_p, s - RING + 1)
                settle(gp)
                gp.tensor_copy(ixg[:, j:j + 1], sloti[:, 0, bass.ds(s, 1)]).then_inc(ixg_s, 1)
                wait(gp, ixg_s, s + 1)
                settle(gp)
                gp.indirect_dma_start(rows[:, j, :], None, hrows,
                                      bass.IndirectOffsetOnAxis(ap=ixg[:, j:j + 1], axis=0)).then_inc(fetch[j], 16)

            def give(s, j, i):
                wait(gp, put[j], 16 * i)
                settle(gp)
                gp.tensor_copy(ixp[:, j:j + 1], sloti[:, 1, bass.ds(s, 1)]).then_inc(ixp_s, 1)
                wait(gp, yo_s, s + 1)
                wait(gp, ixp_s, s + 1)
                settle(gp)
                gp.indirect_dma_start(yrows, bass.IndirectOffsetOnAxis(ap=ixp[:, j:j + 1], axis=0),
                                      yo[:, j, :], None, bounds_check=TOPK * T - 1,
                                      oob_is_err=False).then_inc(put[j], 16)

            def step(s, j, i):
                if not (isinstance(s, int) and s + AHEAD >= NS):
                    get(*later(i, j, AHEAD))
                lo(TT + s, EXPERT_W, j)
                if not (isinstance(s, int) and s == 0):
                    give(*later(i, j, -1))

            for s in range(AHEAD):
                get(s, s, 0)
            over_tiles(gp, step, NS, RING)
            give(NS - 1, RING - 1, NS // RING - 1)

            for b in range(B):
                gp.wait_ge(f_b, b + 1)
                v = yk[:, 0, U * b:U * b + U, :]
                gp.tensor_tensor(v, v, modb[:, b, 3 * D:].unsqueeze(1).to_broadcast([P, U, D]),
                                 ALU.mult).then_inc(f_c, 1)

        @block.scalar
        def _(act):
            act.dma_start(cft[:, :], cf).then_inc(ld_w, 16)
            act.dma_start(cbt[:, :], cb).then_inc(ld_w, 16)
            act.dma_start(wqkv[:, :, :], wqkvT.rearrange("(c p) n -> p c n", p=P)).then_inc(ld_w, 16)
            act.dma_start(wpj[:, :, :], projT.rearrange("(c p) n -> p c n", p=P)).then_inc(ld_w, 16)
            act.dma_start(pb[:, :], proj_b).then_inc(ld_w, 16)
            act.dma_start(gws[:, :, :], gateT.rearrange("(c p) e -> p c e", p=P)).then_inc(ld_g, 16)
            act.dma_start(sw13[:, :, :], sw13T).then_inc(ld_sw, 16)
            act.dma_start(sw2[:, :, :], sw2T).then_inc(ld_sw, 16)
            act.wait_ge(ld_cst, 32)
            act.activation(csig[:, :, :], cts[:, :, :], ACT.Exp, scale=-1.0).then_inc(c_exp, 1)

            def front(b):
                wait(act, hT_p, b + 1)
                if isinstance(b, int) and b == 0:
                    act.wait_ge(pads, 1)
                    act.wait_ge(modT_s, 1)
                wait(act, k_p, b)
                wait(act, hw_s, b)
                for c in range(C):
                    last = act.activation(hT[:, c, WIN:WIN + N], M0[:, c * N:(c + 1) * N], ACT.Identity,
                                          scale=modT[:, 2 + c, bass.ds(b, 1)], bias=modT[:, c, bass.ds(b, 1)])
                last.then_inc(hT_s, 1)
                wait(act, q_p, b + 1)
                wait(act, s_p, U * b)
                for c in range(C):
                    for h in range(GH):
                        last = act.activation(qbd[:, c, :, h], M1[:, c * N:(c + 1) * N], ACT.Copy,
                                              scale=headsel[:, h:h + 1])
                last.then_inc(q_s, 1)
                wait(act, k_p, b + 1)
                for c in range(C):
                    last = act.activation(kT[:, c, WIN:WIN + N], M0[:, c * N:(c + 1) * N], ACT.Copy)
                last.then_inc(k_s, 1)

            def front_v(b):
                wait(act, v_p, b + 1)
                wait(act, z_p, 2 * U * b)
                act.activation(vw[:, :, :], bank[3][:, :], ACT.Copy).then_inc(v_s, 1)

            def main(it, first, final):
                for u in range(U):
                    n = U * it + u
                    wait(act, s_sub, n + 1)
                    act.activation(S[:, u], S[:, u], ACT.Exp).then_inc(s_ex, 1)
                if not first:
                    split(it - 1)
                if not final:
                    front(it + 1)
                for u in range(U):
                    n = U * it + u
                    wait(act, pt_p, n + 1)
                    wait(act, z_p, 2 * (n - U) + 2)
                    act.activation(PT[:, u], SP[u][:, :], ACT.Copy).then_inc(pt_s, 1)
                if not final:
                    front_v(it + 1)

            def split(b):
                wait(act, l2_h, b + 1)
                wait(act, st_h, 16 * b)
                wait(act, xT_p, b)
                act.activation(h3[:, :, 0], h2[:, :, :], ACT.Copy).then_inc(p_hi, 1)
                wait(act, p_r, b + 1)
                act.activation(h3[:, :, 1], hr[:, :, :], ACT.Copy).then_inc(p_mid, 1)
                wait(act, xT_p, b + 1)
                for u in range(U):
                    last = act.activation(xT[:, U * b + u].rearrange("p q t -> p (q t)"), MB[u], ACT.Copy)
                last.then_inc(xT_s, 1)

            front(0)
            front_v(0)
            over(act, main)
            split(B - 1)

            act.wait_ge(lg_s, B)
            act.activation(score[:, :, :], logit[:, :, :], ACT.Exp, scale=-1.0).then_inc(r_exp, 1)

            def silu(n, w, j):
                wait(act, up_p, n + 1)
                wait(act, hid_s, n - 1)
                act.activation(act_s[:, j % 2, 0:w], bank[j % 2][:, 0:w], ACT.Silu).then_inc(silu_s, 1)

            def hi(n, w, j):
                p, k = w
                wait(act, ht_p, n + 1)
                wait(act, y_p, n - 1)
                act.activation(hT3[0:p, j % 2, 0, 0:k], HT(j)[0:p, 0:k], ACT.Copy).then_inc(hi_s, 1)

            def mid(n, w, j):
                p, k = w
                wait(act, res_s, n + 1)
                act.activation(hT3[0:p, j % 2, 1, 0:k], hres[0:p, j % 2, 0:k], ACT.Copy).then_inc(mid_s, 1)

            def shared(t, j, i):
                hi(t, SHARED_W, j)
                if not (isinstance(t, int) and t + 1 == TT):
                    silu(t + 1, SI, j + 1)
                mid(t, SHARED_W, j)

            silu(0, SI, 0)
            over_tiles(act, shared, TT, 2)

            def result(s, j, i):
                wait(act, y_p, TT + s + 1)
                wait(act, put[j], 16 * i)
                if isinstance(s, int) and s == 0:
                    act.wait_ge(sh_s, TT)
                act.activation(yo[:, j, :], YP(j), ACT.Copy).then_inc(yo_s, 1)

            def step(s, j, i):
                hi(TT + s, EXPERT_W, j)
                if not (isinstance(s, int) and s + 1 == NS):
                    silu(TT + s + 1, I, j + 1)
                mid(TT + s, EXPERT_W, j)
                if not (isinstance(s, int) and s == 0):
                    result(*later(i, j, -1))

            silu(TT, I, 0)
            over_tiles(act, step, NS, RING)
            result(NS - 1, RING - 1, NS // RING - 1)

            for b in range(B):
                act.wait_ge(ld_y[b], 16 * TOPK)
                for u in range(U):
                    last = act.activation(yk[:, 0, U * b + u], yk[:, 0, U * b + u], ACT.Copy,
                                          scale=gatew[:, 0, U * b + u:U * b + u + 1])
                last.then_inc(f_a, 1)

        @block.vector
        def _(dve):
            dve.wait_ge(c_exp, 1)
            dve.tensor_scalar(csig[:, :, :], csig[:, :, :], 1.0, None, ALU.add).then_inc(c_den, 1)
            dve.wait_ge(c_den, 1)
            dve.reciprocal(csig[:, :, :], csig[:, :, :]).then_inc(c_inv, 1)
            dve.wait_ge(c_inv, 1)
            dve.tensor_tensor(cts[:, :, :], cts[:, :, :], csig[:, :, :], ALU.mult).then_inc(c_silu, 1)
            dve.wait_ge(mod_p, 1)
            dve.tensor_copy(modrow[:, 0:4 * D], bank[0][0:B, 0:1024])
            dve.tensor_copy(modrow[:, 4 * D:6 * D], bank[1][0:B, 0:512]).then_inc(mod_r, 1)
            dve.wait_ge(mod_r, 1)
            for k in (1, 4):
                dve.tensor_scalar(modrow[:, k * D:(k + 1) * D], modrow[:, k * D:(k + 1) * D], 1.0, None, ALU.add)
            for i, k in enumerate((2, 5)):
                g = modrow[:, k * D:(k + 1) * D]
                dve.tensor_scalar(gtmp[:, i], g, 0.0, 2.0, ALU.is_ge, ALU.mult)
                last = dve.scalar_tensor_tensor(gtmp[:, 2 + i], g, -1.0, g, ALU.mult, ALU.max)
            last.then_inc(g_sgn, 1)
            dve.wait_ge(g_sgn, 1)
            dve.tensor_scalar(gtmp[:, 0:2], gtmp[:, 0:2], -1.0, None, ALU.add)
            dve.tensor_scalar(gtmp[:, 2:4], gtmp[:, 2:4], 0.25, None, ALU.max).then_inc(g_abs, 1)
            dve.wait_ge(g_abs, 1)
            for i, k in enumerate((2, 5)):
                last = dve.tensor_tensor(modrow[:, k * D:(k + 1) * D], gtmp[:, i], gtmp[:, 2 + i], ALU.mult)
            last.then_inc(g_fin, 1)
            dve.wait_ge(modT_p, 1)
            dve.tensor_copy(modT[:, :, :], M0[:, 0:4 * B]).then_inc(modT_s, 1)

            def stats(xt, k):
                for u in range(U):
                    last = dve.bn_stats(bst[:, u], xt(u))
                last.then_inc(ln_st, 1)
                wait(dve, ln_st, k)
                settle(dve)
                for u in range(U):
                    last = dve.bn_aggr(mv[:, u], bst[:, u])
                last.then_inc(ln_mv, 1)
                wait(dve, ln_mv, k)
                dve.tensor_scalar(ve[:, :], mv[:, :, 1], EPS, None, ALU.add).then_inc(ln_ve, 1)

            def ln1(b):
                stats(lambda u: xs[:, U * b + u, :], b + 1)
                wait(dve, ln_rs, b + 1)
                wait(dve, hT_p, b)
                for u in range(U):
                    last = dve.tensor_scalar(xn[:, u], xs[:, U * b + u, :], mv[:, u, 0:1], rstd[:, u:u + 1],
                                             ALU.subtract, ALU.mult)
                last.then_inc(ln_xn, 1)

            def logits(b):
                wait(dve, lg_p, b + 1)
                for u in range(U):
                    last = dve.tensor_reduce(logit[:, U * b + u, :], LG[u].rearrange("p (k e) -> p e k", e=E),
                                             AX.X, ALU.add)
                last.then_inc(lg_s, 1)

            def main(it, first, final):
                for u in range(U):
                    n = U * it + u
                    wait(dve, s_p, n + 1)
                    wait(dve, st_p, n - U + 1)
                    dve.tensor_tensor(ST[:, u], SP[u][:, :].rearrange("p (k j) -> p k j", j=P),
                                      window.unsqueeze(1).to_broadcast([P, NBLK // BPT, P]),
                                      ALU.mult).then_inc(s_m, 1)
                for u in range(U):
                    n = U * it + u
                    wait(dve, st_p, n + 1)
                    sv = SP[u][:, :].rearrange("p (k j) -> p k j", j=KB)
                    dve.tensor_reduce(mx[:, u], sv, AX.X, ALU.max).then_inc(s_mx, 1)
                    wait(dve, s_mx, n + 1)
                    wait(dve, pt_p, n - U + 1)
                    dve.tensor_tensor(S[:, u], sv, mx[:, u, :].unsqueeze(2).to_broadcast([P, NBLK, KB]),
                                      ALU.subtract).then_inc(s_sub, 1)
                if not final:
                    if first:
                        dve.wait_ge(ld_x1, 16)
                    ln1(it + 1)
                for u in range(U):
                    n = U * it + u
                    wait(dve, s_ex, n + 1)
                    dve.tensor_reduce(rs[:, u], S[:, u], AX.X, ALU.add).then_inc(s_sum, 1)
                    wait(dve, s_sum, n + 1)
                    dve.reciprocal(ri[:, u], rs[:, u]).then_inc(s_ri, 1)
                if not first:
                    logits(it - 1)
                for u in range(U):
                    n = U * it + u
                    for z in range(2):
                        wait(dve, z_p, 2 * n + z + 1)
                        dve.tensor_tensor(Z[:, z], ZP[:, :].rearrange("p (k h) -> p k h", h=GH),
                                          headsel.unsqueeze(1).to_broadcast([P, NBLK // 4 * QB, GH]),
                                          ALU.mult).then_inc(z_s, 1)
                        wait(dve, z_s, 2 * n + z + 1)
                        wait(dve, pr_p, n - U + 1)
                        ov = OT[:, u].rearrange("p c (q r t) -> p r q c t", q=2, r=BPT)
                        zv = Z[:, z].rearrange("p (r q c t) h -> p r q c t h", r=2, q=2, c=C)
                        for rr in range(2):
                            last = dve.tensor_reduce(ov[:, 2 * z + rr], zv[:, rr], AX.X, ALU.add)
                    last.then_inc(o_s, 1)
                if first:
                    dve.wait_ge(mod_ld, 16)
                for u in range(U):
                    n = U * it + u
                    wait(dve, pr_p, n + 1)
                    dve.tensor_tensor(ao[:, u], SP[u][:, 512:512 + D], modb[:, it, 0:D], ALU.mult).then_inc(ga_s, 1)
                    wait(dve, ga_s, n + 1)
                    dve.tensor_tensor(xs[:, n, :], xs[:, n, :], ao[:, u], ALU.add).then_inc(x1_s, 1)
                wait(dve, x1_s, U * it + U)
                settle(dve)
                for u in range(U):
                    last = dve.bn_stats(bst2[:, u], xs[:, U * it + u, :])
                last.then_inc(l2_st, 1)
                wait(dve, l2_st, it + 1)
                settle(dve)
                for u in range(U):
                    last = dve.bn_aggr(mv2[:, u], bst2[:, u])
                last.then_inc(l2_mv, 1)
                wait(dve, l2_mv, it + 1)
                dve.tensor_scalar(ve2[:, :], mv2[:, :, 1], EPS, None, ALU.add).then_inc(l2_ve, 1)
                wait(dve, l2_rs, it + 1)
                wait(dve, p_r, it)
                for u in range(U):
                    last = dve.tensor_scalar(h2[:, u], xs[:, U * it + u, :], mv2[:, u, 0:1], rstd2s[:, u:u + 1],
                                             ALU.subtract, ALU.mult)
                last.then_inc(l2_xn, 1)

            dve.wait_ge(ld_x0, 16)
            ln1(0)
            dve.wait_ge(ld_g, 16)
            for k in range(PARTS):
                dve.tensor_copy(gw3[:, :, k, :], gws[:, :, :]).then_inc(gw_s, 1)
                if k < PARTS - 1:
                    dve.wait_ge(gw_s, 2 * k + 1)
                    dve.tensor_tensor(gws[:, :, :], gws[:, :, :], gw3[:, :, k, :], ALU.subtract).then_inc(gw_s, 1)
                    dve.wait_ge(gw_s, 2 * k + 2)
            over(dve, main)
            logits(B - 1)

            links = [0]

            def link(ins):
                links[0] += 1
                ins.then_inc(rt, 1)
                dve.wait_ge(rt, links[0])

            dve.wait_ge(r_exp, 1)
            link(dve.tensor_scalar(score[:, :, :], score[:, :, :], 1.0, None, ALU.add))
            link(dve.reciprocal(score[:, :, :], score[:, :, :]))
            revb = rev.unsqueeze(1).to_broadcast([P, TT, E])
            for k in range(TOPK):
                link(dve.tensor_reduce(top[:, k], score[:, :, :], AX.X, ALU.max))
                link(dve.tensor_tensor(cand[:, :, :], score[:, :, :],
                                       top[:, k].unsqueeze(2).to_broadcast([P, TT, E]), ALU.is_equal))
                link(dve.tensor_tensor(cand[:, :, :], cand[:, :, :], revb, ALU.mult))
                link(dve.tensor_reduce(rtop[:, k], cand[:, :, :], AX.X, ALU.max))
                link(dve.tensor_tensor(oh[:, k], rtop[:, k].unsqueeze(2).to_broadcast([P, TT, E]), revb,
                                       ALU.is_equal))
                if k == 0:
                    link(dve.scalar_tensor_tensor(score[:, :, :], oh[:, k], -2.0, score[:, :, :],
                                                  ALU.mult, ALU.add))
            dve.tensor_tensor(ohb[:, 0:TT, :], oh[:, 0], oh[:, 1], ALU.add).then_inc(ohb_s, 1)
            link(dve.tensor_tensor(den[:, :], top[:, 0], top[:, 1], ALU.add))
            link(dve.reciprocal(den[:, :], den[:, :]))
            dve.tensor_tensor(gatew[:, :, :], top[:, :, :], den[:, :].unsqueeze(1).to_broadcast([P, TOPK, TT]),
                              ALU.mult)
            dve.wait_ge(rank_p, 1)
            rank = bank[0][:, 0:TT * E].rearrange("p (t e) -> p t e", e=E)
            link(dve.tensor_scalar(cnti[:, :], bank[0][:, TT * E:TT * E + E], float(P - 1), None, ALU.add))
            link(dve.tensor_scalar(cnti[:, :], cnti[:, :], P.bit_length() - 1, None, ALU.arith_shift_right))
            link(dve.tensor_copy(cnt[:, 0], cnti[:, :]))
            link(dve.tensor_tensor_scan(cnt[:, 1], one, cnt[:, 0], 0.0, ALU.mult, ALU.add))
            link(dve.tensor_tensor(cnt[:, 2], cnt[:, 1], cnt[:, 0], ALU.subtract))
            link(dve.tensor_scalar(cnt[:, 3], cnt[:, 2], float(P), None, ALU.mult))
            link(dve.tensor_tensor(cand[:, :, :], rank, cnt[:, 3].unsqueeze(1).to_broadcast([P, TT, E]), ALU.add))
            for k in range(TOPK):
                link(dve.tensor_tensor(oh[:, k], oh[:, k], cand[:, :, :], ALU.mult))
            link(dve.tensor_reduce(pos[:, :], oh[:, :, :, :].rearrange("p k t e -> p (k t) e"), AX.X, ALU.add))
            link(dve.tensor_copy(posi[:, 0], pos[:, :]))
            link(dve.tensor_scalar(posi[:, 1], posi[:, 0], P - 1, None, ALU.bitwise_and))
            link(dve.tensor_scalar(posi[:, 2], posi[:, 0], P.bit_length() - 1, None, ALU.arith_shift_right))
            link(dve.tensor_copy(posf[:, :, :], posi[:, 1:3]))
            TK = TOPK * TT
            dve.tensor_tensor(lane_oh[:, :, :], lane.unsqueeze(1).to_broadcast([P, TK, P]),
                              posf[:, 0].unsqueeze(2).to_broadcast([P, TK, P]), ALU.is_equal)
            link(dve.tensor_tensor(tile_oh[:, :, :], tileno.unsqueeze(1).to_broadcast([P, TK, NS]),
                                   posf[:, 1].unsqueeze(2).to_broadcast([P, TK, NS]), ALU.is_equal))
            dve.tensor_tensor(val[:, :, 0], tile_oh[:, :, :], turn.unsqueeze(2).to_broadcast([P, TK, NS]), ALU.mult)
            dve.tensor_scalar(val[:, :, 1], tile_oh[:, :, :], row1, None, ALU.mult).then_inc(val_s, 1)
            link(dve.tensor_tensor(owner[:, :, :], tileno.unsqueeze(2).to_broadcast([P, NS, E]),
                                   cnt[:, 1].unsqueeze(1).to_broadcast([P, NS, E]), ALU.is_ge))
            link(dve.tensor_reduce(slot[:, 0], owner[:, :, :], AX.X, ALU.add))
            link(dve.tensor_scalar(expert[:, :], slot[:, 0], float(E - 1), None, ALU.min))
            dve.wait_ge(slot_p, 1)
            who = bank[1][:, 0:2 * NS].rearrange("p (k s) -> p k s", k=2)
            link(dve.tensor_copy(slot[:, 0:2], who))
            link(dve.scalar_tensor_tensor(slot[:, 2], slot[:, 0], float(P), slot[:, 1], ALU.mult, ALU.add))
            link(dve.tensor_scalar(slot[:, 3], slot[:, 1], 0.0, float(NONE), ALU.is_equal, ALU.mult))
            dve.tensor_scalar(sloti[:, 0], slot[:, 2], -1.0, 0.0, ALU.add, ALU.max)
            link(dve.scalar_tensor_tensor(sloti[:, 1], slot[:, 2], -1.0, slot[:, 3], ALU.add, ALU.add))
            dve.tensor_scalar(sloti[:, 0], sloti[:, 0], T - 1, None, ALU.bitwise_and).then_inc(routed, 1)

            def hidden(n, w, boff, j):
                wait(dve, silu_s, n + 1)
                wait(dve, ht_p, n - 1)
                dve.tensor_tensor(hid[:, j % 2, 0:w], act_s[:, j % 2, 0:w], bank[j % 2][:, boff:boff + w],
                                  ALU.mult).then_inc(hid_s, 1)

            def rest(n, w, j):
                p, k = w
                wait(dve, hi_s, n + 1)
                wait(dve, lo_s, n - 1)
                dve.tensor_tensor(hres[0:p, j % 2, 0:k], HT(j)[0:p, 0:k], hT3[0:p, j % 2, 0, 0:k],
                                  ALU.subtract).then_inc(res_s, 1)

            def base(t, j, b):
                wait(dve, y_p, t + 1)
                dve.tensor_tensor(yo[:, j, :], YP(j), modb[:, b, 3 * D:], ALU.mult).then_inc(y_s, 1)
                wait(dve, y_s, t + 1)
                dve.tensor_tensor(xs[:, t, :], xs[:, t, :], yo[:, j, :], ALU.add).then_inc(sh_s, 1)

            def shared(t, j, i):
                if not (isinstance(t, int) and t + 1 == TT):
                    hidden(t + 1, SI, 512, j + 1)
                rest(t, SHARED_W, j)
                if not (isinstance(t, int) and t == 0):
                    base(t - 1, 1 - j, i if j == 1 else i - 1)

            hidden(0, SI, 512, 0)
            over_tiles(dve, shared, TT, 2)
            base(TT - 1, 1, B - 1)

            def rows_turned(s, j, i):
                wait(dve, rT_p, s + 1)
                wait(dve, up_p, TT + s - 1)
                dve.tensor_copy(rT[:, j % 2].rearrange("p q t -> p (q t)"), RTP(j)).then_inc(rT_s, 1)

            def step(s, j, i):
                if not (isinstance(s, int) and s + 1 == NS):
                    hidden(TT + s + 1, I, I, j + 1)
                rest(TT + s, EXPERT_W, j)
                if not (isinstance(s, int) and s + 2 >= NS):
                    rows_turned(*later(i, j, 2))

            def finish(b):
                dve.wait_ge(f_c, b + 1)
                v = xs[:, U * b:U * b + U, :]
                dve.tensor_tensor(v, v, yk[:, 0, U * b:U * b + U, :], ALU.add).then_inc(f_d, 1)

            rows_turned(0, 0, 0)
            hidden(TT, I, I, 0)
            rows_turned(1, 1, 0)
            over_tiles(dve, step, NS, RING)

            for b in range(B):
                dve.wait_ge(f_a, b + 1)
                for u in range(U):
                    k = U * b + u
                    last = dve.scalar_tensor_tensor(yk[:, 0, k], yk[:, 1, k], gatew[:, 1, k:k + 1], yk[:, 0, k],
                                                    ALU.mult, ALU.add)
                last.then_inc(f_b, 1)
                if b:
                    finish(b - 1)
            finish(B - 1)

        @block.tensor
        def _(pe):
            pe.wait_ge(c_silu, 1)
            for j in range(3):
                o = bank[j // 2][0:B, (j % 2) * 512:(j % 2 + 1) * 512]
                for c in range(C):
                    last = pe.matmul(o, cts[:, c, :], wms[:, c, j * 512:(j + 1) * 512], start=c == 0, stop=c == C - 1)
            last.then_inc(mod_p, 1)
            pe.wait_ge(ld_w, 80)
            pe.wait_ge(g_fin, 1)
            for k in range(4):
                last = pe.transpose(M0[:, k * B:(k + 1) * B], modrow[:, k * P:(k + 1) * P], ident[0:B, 0:B])
            last.then_inc(modT_p, 1)

            def front(b):
                wait(pe, ln_xn, b + 1)
                wait(pe, v_s, b)
                wait(pe, lg_s, b - 1)
                if isinstance(b, int) and b == 0:
                    pe.wait_ge(modT_s, 1)
                for c in range(C):
                    for u in range(U):
                        last = pe.transpose(M0[:, c * N + u * P:c * N + (u + 1) * P],
                                            xn[:, u, c * P:(c + 1) * P], ident)
                last.then_inc(hT_p, 1)
                wait(pe, hT_s, b + 1)
                for name, m, off, done in (("q", M1, 0, q_p), ("k", M0, D, k_p)):
                    for c in range(C):
                        for k in range(C):
                            last = pe.matmul(m[:, c * N:(c + 1) * N], wqkv[:, k, off + c * P:off + (c + 1) * P],
                                             hT[:, k, WIN:WIN + N], start=k == 0, stop=k == C - 1)
                    last.then_inc(done, 1)

            def front_v(b):
                wait(pe, hw_s, b + 1)
                wait(pe, k_s, b + 1)
                wait(pe, q_s, b + 1)
                for w in range(N // (QB * BPT)):
                    for k in range(C):
                        o = bank[3][:, w * D:(w + 1) * D]
                        lhsT = hw[:, k, BPT * w:BPT * (w + 1), :]
                        last = pe.matmul(o, lhsT, wqkv[:, k, 2 * D:3 * D], start=k == 0, stop=k == C - 1)
                last.then_inc(v_p, 1)

            def scores(it, u):
                n = U * it + u
                wait(pe, q_s, it + 1)
                wait(pe, k_s, it + 1)
                wait(pe, ga_s, n - U + 1)
                for s in range(2):
                    pe.matmul(SP[u][:, s * 512:(s + 1) * 512], identb, addmask(u), start=True, stop=False,
                              skip_group_check=True)
                for c in range(C):
                    for b in range(BL):
                        for s in range(2):
                            q0 = u * P + b * QB
                            r, o = b % BPT, ((s * C + c) * 2 + b // BPT) * P
                            last = pe.matmul(SP[u][KB * r:KB * (r + 1), o:o + P],
                                             kT[GC * s:GC * (s + 1), c, q0:q0 + KB],
                                             qbd[GC * s:GC * (s + 1), c, q0:q0 + QB, :],
                                             start=False, stop=True, skip_group_check=True)
                last.then_inc(s_p, 1)

            def turn_s(it, u):
                wait(pe, s_m, U * it + u + 1)
                for j in range(NBLK // BPT):
                    last = pe.transpose(SP[u][:, j * P:(j + 1) * P], ST[:, u, j, :], ident)
                last.then_inc(st_p, 1)

            def turn_p(it, u):
                wait(pe, s_nm, U * it + u + 1)
                for j in range(NBLK // BPT):
                    last = pe.transpose(SP[u][:, j * P:(j + 1) * P], S[:, u, BPT * j:BPT * (j + 1), :], ident)
                last.then_inc(pt_p, 1)

            def times_v(it, u, z):
                n = U * it + u
                wait(pe, pt_s, n + 1)
                wait(pe, v_s, it + 1)
                wait(pe, z_s, 2 * n + z)
                for q in range(2):
                    for c in range(C):
                        for s in range(2):
                            for rr in range(2):
                                r, g = 2 * z + rr, 2 * c + s
                                o = rr * 512 + (q * C + c) * P
                                last = pe.matmul(ZP[GC * s:GC * (s + 1), o:o + P],
                                                 vw[KB * r:KB * (r + 1), 2 * u + q, g * GC:(g + 1) * GC],
                                                 PT[KB * r:KB * (r + 1), u, (s * C + c) * 2 + q, :],
                                                 start=True, stop=True, skip_group_check=True)
                last.then_inc(z_p, 1)

            def project(it, u):
                n = U * it + u
                wait(pe, o_s, n + 1)
                o = SP[u][:, 512:512 + D]
                pe.matmul(o, ones_row[:, :], pb[:, :], start=True, stop=False)
                for c in range(C):
                    last = pe.matmul(o, OT[:, u, c, :], wpj[:, c, :], start=False, stop=c == C - 1)
                last.then_inc(pr_p, 1)

            def main(it, first, final):
                scores(it, 0)
                scores(it, 1)
                turn_s(it, 0)
                turn_s(it, 1)
                if not first:
                    split(it - 1)
                if not final:
                    front(it + 1)
                turn_p(it, 0)
                turn_p(it, 1)
                times_v(it, 0, 0)
                times_v(it, 0, 1)
                times_v(it, 1, 0)
                times_v(it, 1, 1)
                project(it, 0)
                if not final:
                    front_v(it + 1)
                project(it, 1)

            def split(b):
                wait(pe, p_lo, b + 1)
                wait(pe, v_s, b + 2 if not (isinstance(b, int) and b + 2 > B) else B)
                for u in range(U):
                    for q in range(PARTS * C):
                        last = pe.transpose(MB[u][:, q * P:(q + 1) * P],
                                            h3[:, u, q // C, (q % C) * P:(q % C + 1) * P], identb)
                last.then_inc(xT_p, 1)
                wait(pe, xT_s, b + 1)
                for u in range(U):
                    for q in range(PARTS * C):
                        last = pe.matmul(LG[u], xT[:, U * b + u, q, :], gw3[:, q % C].rearrange("p k e -> p (k e)"),
                                         start=q == 0, stop=q == PARTS * C - 1)
                last.then_inc(lg_p, 1)

            front(0)
            front_v(0)
            over(pe, main)
            split(B - 1)

            pe.wait_ge(ohb_s, 1)
            pe.matmul(bank[0][:, 0:(TT + 1) * E], before, ohb[:, :, :].rearrange("p t e -> p (t e)"), start=True, stop=False,
                      skip_group_check=True)
            for t in range(TT):
                last = pe.matmul(bank[0][:, (t + 1) * E:(TT + 1) * E].rearrange("p (t e) -> p t e", e=E), onesb,
                                 ohb[:, t, :].unsqueeze(1).to_broadcast([P, TT - t, E]), start=False, stop=t == TT - 1,
                                 skip_group_check=True)
            last.then_inc(rank_p, 1)
            pe.wait_ge(val_s, 1)
            for k in range(TOPK * TT):
                last = pe.matmul(bank[1][:, 0:2 * NS], lane_oh[:, k, :], val[:, k].rearrange("p v s -> p (v s)"),
                                 start=k == 0, stop=k == TOPK * TT - 1)
            last.then_inc(slot_p, 1)

            def turn_hidden(n, k, p, j):
                wait(pe, hid_s, n + 1)
                wait(pe, res_s, n - 1)
                for q in range(k):
                    last = pe.transpose(HT(j)[0:p, q, :], hid[:, j % 2, q * p:(q + 1) * p], ident)
                last.then_inc(ht_p, 1)

            def up_shared(t, j):
                wait(pe, hid_s, t - 1)
                for half in range(2):
                    for q in range(PARTS * C):
                        last = pe.matmul(bank[j % 2][:, half * 512:half * 512 + SI], xT[:, t, q, :],
                                         sw13[:, q % C, half * SI:(half + 1) * SI],
                                         start=q == 0, stop=q == PARTS * C - 1)
                last.then_inc(up_p, 1)

            def down_shared(t, j):
                wait(pe, lo_s, t + 1)
                wait(pe, y_s, t - 1)
                last_k = SI - (SK - 1) * P
                for k in range(SK):
                    p = P if k < SK - 1 else last_k
                    for q in range(PARTS):
                        last = pe.matmul(YP(j), hT3[0:p, j % 2, q, k, :], sw2[0:p, k, :],
                                         start=k == 0 and q == 0, stop=k == SK - 1 and q == PARTS - 1)
                last.then_inc(y_p, 1)

            def shared(t, j, i):
                turn_hidden(t, SK, P, j)
                if not (isinstance(t, int) and t + 1 == TT):
                    up_shared(t + 1, j + 1)
                if not (isinstance(t, int) and t == 0):
                    down_shared(t - 1, j + 1)

            pe.wait_ge(routed, 1)
            pe.wait_ge(ld_sw, 32)
            up_shared(0, 0)
            over_tiles(pe, shared, TT, 2)
            down_shared(TT - 1, 1)

            def turn_rows(s, j, i):
                wait(pe, fetch[j], 16 * (i + 1))
                wait(pe, rT_s, s - 1)
                if isinstance(s, int) and s < 2:
                    pe.wait_ge(hid_s, TT)
                for q in range(PARTS * C):
                    last = pe.transpose(RTP(j)[:, q * P:(q + 1) * P], rows[:, j, q * P:(q + 1) * P], identb)
                last.then_inc(rT_p, 1)

            def tile_expert(s):
                return pe.value_load(expert[0:1, bass.ds(s, 1)], min_val=0, max_val=E - 1)

            def up(s, j):
                e = tile_expert(s)
                wait(pe, rT_s, s + 1)
                wait(pe, hid_s, TT + s - 1)
                for q in range(PARTS * C):
                    last = pe.matmul(bank[j % 2][:, 0:2 * I], rT[:, j % 2, q, :], w13[:, q % C, bass.ds(e, 1), :],
                                     start=q == 0, stop=q == PARTS * C - 1)
                last.then_inc(up_p, 1)

            def down(s, j):
                e = tile_expert(s)
                wait(pe, lo_s, TT + s + 1)
                if isinstance(s, int) and s < 2:
                    pe.wait_ge(y_s, TT + s - 1)
                else:
                    wait(pe, yo_s, s - 1)
                for k in range(2):
                    for q in range(PARTS):
                        last = pe.matmul(YP(j), hT3[0:IH, j % 2, q, k, :], w2[:, k, bass.ds(e, 1), :],
                                         start=k == 0 and q == 0, stop=k == 1 and q == PARTS - 1)
                last.then_inc(y_p, 1)

            def step(s, j, i):
                turn_hidden(TT + s, 2, IH, j)
                if not (isinstance(s, int) and s + 1 == NS):
                    up(s + 1, j + 1)
                if not (isinstance(s, int) and s + 2 >= NS):
                    turn_rows(*later(i, j, 2))
                if not (isinstance(s, int) and s == 0):
                    down(s - 1, j + 1)

            pe.wait_ge(ld_ew, 32)
            turn_rows(0, 0, 0)
            up(0, 0)
            turn_rows(1, 1, 0)
            over_tiles(pe, step, NS, RING)
            down(NS - 1, NS - 1)


_OUT = (B, N, D)


def kernel(**inputs):
    import numpy as np
    import ml_dtypes
    import concourse.bacc as bacc
    from concourse.bass_utils import run_bass_kernel_spmd as run

    a = {k: np.asarray(v) for k, v in inputs.items()}

    row = np.arange(P)
    t, h = row // GH, row % GH
    j = np.arange(KB)
    d = j[None, :] - WIN - t[:, None]
    inside = (d >= -WIN) & (d < WIN)
    m = np.where(inside, (WIN - np.abs(d) / 2.0) / WIN * HD ** -0.5, 1.0)
    cf = np.zeros((P, FCW), np.float32)
    cf[:, slice(*FC["ident"])] = np.eye(P)
    cf[:, slice(*FC["window"])] = np.tile(m.T, (BPT, 1))
    cf[:, slice(*FC["headsel"])] = ((row % GC) // HD)[:, None] == np.arange(GH)[None, :]
    cf[:, slice(*FC["nhalf"])] = -0.5
    cf[:, slice(*FC["rev"])] = E - np.arange(E)
    cf[:, slice(*FC["lane"])] = row
    cf[:, slice(*FC["tile"])] = np.arange(NS)
    cf[:, slice(*FC["turn"])] = np.arange(TOPK * TT)
    cf[:, slice(*FC["row1"])] = row[:, None] + 1
    cf[:, slice(*FC["one"])] = 1.0
    cb = np.zeros((P, BCW), np.float32)
    cb[:, 0:P] = np.eye(P)
    cb[:, BCW - 2 * P:BCW - P] = row[:, None] < row[None, :]
    cb[:, BCW - P:] = 1.0
    for u in range(U):
        key = u * P + QB * np.arange(BL)[:, None] + j[None, :] - WIN
        ok = inside.T[None, :, :] & ((key >= 0) & (key < N))[:, :, None]
        ok = ok.reshape(2, P, P).transpose(1, 0, 2)
        ok = np.broadcast_to(ok[:, None], (P, C, 2, P))
        cb[:, P + u * 4 * P:P + (u + 1) * 4 * P] = np.where(ok, 0.0, -1e30).reshape(P, -1)
    cb = cb.astype(ml_dtypes.bfloat16)

    w13 = np.concatenate([a["L0_ffn_w1"], a["L0_ffn_w3"]], axis=1)
    sw13 = np.concatenate([a["L0_ffn_sw1"], a["L0_ffn_sw3"]], axis=0)
    sw2 = np.zeros((SK * P, D), a["L0_ffn_sw2"].dtype)
    sw2[:SI] = a["L0_ffn_sw2"].T
    arrays = {
        "gateT": a["L0_ffn_gate_w"].T,
        "w13T": w13.reshape(E, 2 * I, C, P).transpose(3, 2, 0, 1),
        "w2T": a["L0_ffn_w2"].reshape(E, D, 2, IH).transpose(3, 2, 0, 1),
        "sw13T": sw13.reshape(2 * SI, C, P).transpose(2, 1, 0),
        "sw2T": sw2.reshape(SK, P, D).transpose(1, 0, 2),
        "x": a["L0_attn_x"].reshape(T, D),
        "wqkvT": a["L0_attn_qkv_w"].T,
        "projT": a["L0_attn_proj_w"].T,
        "proj_b": a["L0_attn_proj_b"].reshape(1, D),
        "cT": a["L0_c"].T,
        "wmod": a["L0_wmod"],
        "cf": cf,
        "cb": cb,
    }
    arrays = {k: np.ascontiguousarray(v) for k, v in arrays.items()}
    nc = bacc.Bacc("TRN2", target_bir_lowering=False, num_devices=1)
    args = {k: nc.dram_tensor(k, v.shape, mybir.dt.from_np(v.dtype), kind="ExternalInput").ap()
            for k, v in arrays.items()}
    out = nc.dram_tensor("out", (T, D), F32, kind="ExternalOutput").ap()
    build(nc, **args, out=out)
    r = run(nc, [arrays], core_ids=[0])
    return r.results[0]["out"].reshape(_OUT)
```

```python
from contextlib import ExitStack

import concourse.bass as bass
import numpy as np
from concourse import mybir

F32 = mybir.dt.float32
I32 = mybir.dt.int32
BF16 = mybir.dt.bfloat16
ALU = mybir.AluOpType
ACT = mybir.ActivationFunctionType
AX = mybir.AxisListType

B, N, D = 8, 256, 256
T = B * N
P = 128
C = D // P
TT = T // P
U = N // P
HEADS, HD, WIN = 32, 8, 8

QB = 16
KB = 2 * QB
GH = P // QB
GC = GH * HD
G = D // GC
BL = P // QB
NBLK = G * BL
BPT = P // KB
NQ = BPT
PADN = WIN + N + WIN
EPS = 1e-5

E, I, SI, TOPK = 16, 176, 352, 2
IH = I // 2
SK = -(-SI // P)
PARTS = 3
NS = T * TOPK // P + E
RING = 4
AHEAD = 3
SHARED_W = (P, SK)
EXPERT_W = (IH, 2)
NONE = 8192

FC = {}
_w = 0
for _n, _k in (("ident", P), ("window", P), ("headsel", GH), ("nhalf", 2), ("rev", E), ("lane", P), ("tile", NS),
               ("turn", TOPK * TT), ("row1", 1), ("one", E)):
    FC[_n] = (_w, _w + _k)
    _w += _k
FCW = _w
BCW = P + 2 * 4 * P + 2 * P


def build(nc, x, wqkvT, projT, proj_b, cT, wmod, gateT, w13T, w2T, sw13T, sw2T, cf, cb, out):
    ctx = ExitStack()
    with ctx:
        def sb(name, shape, dt=F32):
            return ctx.enter_context(nc.sbuf_tensor(name, shape, dt))

        def sem(name):
            return ctx.enter_context(nc.semaphore(name))

        class Region:

            def __init__(self, tensor):
                self.tensor, self.at = tensor, 0

            def take(self, pattern, shape, dt=F32):
                n = int(np.prod([v for v in shape])) * (2 if dt == BF16 else 4) // 4
                v = self.tensor[:, self.at:self.at + n]
                self.at += n
                assert self.at <= self.tensor.shape[1]
                if dt != F32:
                    v = v.bitcast(dt)
                if len(shape) == 1:
                    return v
                names = pattern.split()
                return v.rearrange(f"p ({pattern}) -> p {pattern}", **dict(zip(names[1:], shape[1:])))

        first_region = sb("first_region", [P, C * 6 * D])
        setup = Region(first_region)
        picks = Region(first_region)
        second_region = sb("second_region", [P, 6720])
        attn = Region(second_region)
        late = Region(second_region)
        xs = sb("xs", [P, TT, D])
        cft = sb("cft", [P, FCW])
        cbt = sb("cbt", [P, BCW], BF16)
        wqkv = attn.take("c n", (C, 3 * D,))
        wpj = attn.take("c n", (C, D,))
        pb = sb("pb", [1, D])
        ones_row = sb("ones_row", [1, P])
        cts = sb("cts", [P, C, B])
        csig = sb("csig", [P, C, B])
        wms = setup.take("c n", (C, 6 * D,))
        modrow = sb("modrow", [B, 6 * D])
        gtmp = sb("gtmp", [B, 4, D])
        modT = sb("modT", [P, 4, B])
        modb = sb("modb", [P, B, 4 * D])

        bst2 = sb("bst2", [P, U, 6])
        mv2 = sb("mv2", [P, U, 2])
        ve2 = sb("ve2", [P, U])
        rstd2s = sb("rstd2s", [P, U])
        bst = sb("bst", [P, U, 6])
        mv = sb("mv", [P, U, 2])
        ve = sb("ve", [P, U])
        rstd = sb("rstd", [P, U])
        xn = attn.take("u d", (U, D,))
        hT = attn.take("c n", (C, PADN,))
        hw = attn.take("c b j", (C, N // QB, KB,))
        region = sb("region", [P, C * N * GH + 4 * 2048])
        at = C * N * GH
        qbd = region[:, 0:at].rearrange("p (c n h) -> p c n h", c=C, h=GH)
        kT = attn.take("c n", (C, PADN,))
        vw = attn.take("w d", (N // (QB * BPT), D,))
        ST = region[:, at:at + 2048].rearrange("p (u k j) -> p u k j", u=U, j=P)
        S = region[:, at + 2048:at + 4096].rearrange("p (u k j) -> p u k j", u=U, j=KB)
        mx = sb("mx", [P, U, NBLK])
        rs = sb("rs", [P, U, NBLK])
        ri = sb("ri", [P, U, NBLK])
        PT = region[:, at + 4096:at + 6144].rearrange("p (u k j) -> p u k j", u=U, j=P)
        Z = region[:, at + 6144:at + 8192].rearrange("p (z k h) -> p z k h", z=NQ, h=GH)
        w13n, w2n = C * E * SI // 2, 2 * E * D // 2
        w13 = region[:, 0:w13n].bitcast(BF16).rearrange("p (c e i) -> p c e i", c=C, e=E)
        w2 = region[0:IH, w13n:w13n + w2n].bitcast(BF16).rearrange("p (k e d) -> p k e d", k=2, e=E)
        yk = region[:, 0:TOPK * TT * D].rearrange("p (k t d) -> p k t d", k=TOPK, t=TT)
        OT = attn.take("u c t", (U, C, P,))
        ao = attn.take("u d", (U, D,))

        h2 = sb("h2", [P, U, D])
        hr = sb("hr", [P, U, D])
        h3 = sb("h3", [P, U, PARTS, D], BF16)
        xT = sb("xT", [P, TT, PARTS * C, P], BF16)
        gws = sb("gws", [P, C, E])
        gwr = sb("gwr", [P, C, E])
        gw3 = sb("gw3", [P, C, PARTS, E], BF16)
        sw13 = sb("sw13", [P, C, 2 * SI], BF16)
        sw2 = sb("sw2", [P, SK, D], BF16)
        logit = sb("logit", [P, TT, E])
        score = sb("score", [P, TT, E])
        cand = sb("cand", [P, TT, E])
        oh = sb("oh", [P, TOPK, TT, E])
        ohb = sb("ohb", [P, TT + 1, E], BF16)
        top = sb("top", [P, TOPK, TT])
        rtop = sb("rtop", [P, TOPK, TT])
        gatew = sb("gatew", [P, TOPK, TT])
        den = sb("den", [P, TT])
        cnt = sb("cnt", [P, 4, E])
        cnti = sb("cnti", [P, E], I32)
        pos = sb("pos", [P, TOPK * TT])
        posi = sb("posi", [P, 3, TOPK * TT], I32)
        posf = sb("posf", [P, 2, TOPK * TT])
        lane_oh = picks.take("k l", (TOPK * TT, P,), BF16)
        tile_oh = picks.take("k s", (TOPK * TT, NS,), BF16)
        val = late.take("k v s", (TOPK * TT, 2, NS,), BF16)
        owner = late.take("s e", (NS, E,))
        slot = sb("slot", [P, 4, NS])
        sloti = sb("sloti", [P, 2, NS], I32)
        expert = sb("expert", [P, NS], I32)
        ixg = sb("ixg", [P, RING], I32)
        ixp = sb("ixp", [P, RING], I32)
        rows = late.take("j n", (RING, PARTS * D,), BF16)
        rT = late.take("j q t", (2, PARTS * C, P,), BF16)
        act_s = late.take("j w", (2, SI,))
        hid = sb("hid", [P, 2, SK * P])
        hres = late.take("j k t", (2, SK, P,))
        hT3 = sb("hT3", [P, 2, PARTS, SK, P], BF16)
        yo = sb("yo", [P, RING, D])

        ident = cft[:, FC["ident"][0]:FC["ident"][1]]
        window = cft[:, FC["window"][0]:FC["window"][1]]
        headsel = cft[:, FC["headsel"][0]:FC["headsel"][1]]
        nhalf = cft[:, FC["nhalf"][0]:FC["nhalf"][1]]
        rev, lane, tileno, turn, row1, one = (cft[:, FC[n][0]:FC[n][1]] for n in (
            "rev", "lane", "tile", "turn", "row1", "one"))
        identb = cbt[:, 0:P]
        before = cbt[:, BCW - 2 * P:BCW - P]
        onesb = cbt[:, BCW - P:BCW]

        def addmask(u):
            return cbt[:, P + u * 4 * P:P + (u + 1) * 4 * P]

        bank = [ctx.enter_context(nc.psum_tensor(f"bank{i}", [P, 1024], F32)) for i in range(4)]
        SP = [bank[0], bank[1]]
        ZP = bank[2]
        M0 = bank[3][:, 0:512]
        M1 = bank[3][:, 512:1024]

        MB = [ZP[:, u * 512:u * 512 + PARTS * D // 2].bitcast(BF16) for u in range(U)]
        LG = [ZP[:, u * 512 + PARTS * D // 2:u * 512 + PARTS * D // 2 + PARTS * E] for u in range(U)]

        def HT(j):
            return bank[2][:, (j % 2) * 512:(j % 2) * 512 + SK * P].rearrange("p (k t) -> p k t", t=P)

        def YP(j):
            return bank[3][:, (j % 2) * 512:(j % 2) * 512 + D]

        def RTP(j):
            return bank[j % 2][:, 512:512 + PARTS * D // 2].bitcast(BF16)

        moddram = nc.dram_tensor("moddram", [B, 6 * D], F32, kind="Internal").ap()

        hrows = nc.dram_tensor("hrows", [T, PARTS * D], BF16, kind="Internal").ap()
        yrows = nc.dram_tensor("yrows", [TOPK * T, D], F32, kind="Internal").ap()

        l2_st, l2_mv, l2_ve, l2_rs, l2_xn, l2_mu, l2_h = (sem("l2_" + n) for n in (
            "st", "mv", "ve", "rs", "xn", "mu", "h"))
        p_hi, p_r, p_mid, p_lo, xT_p, xT_s, lg_p, lg_s, st_h = (sem(n) for n in (
            "p_hi", "p_r", "p_mid", "p_lo", "xT_p", "xT_s", "lg_p", "lg_s", "st_h"))
        ld_g, ld_sw, ld_ew, gw_s = (sem(n) for n in ("ld_g", "ld_sw", "ld_ew", "gw_s"))
        r_exp, rt, rank_p, slot_p, routed, ohb_s = (sem(n) for n in (
            "r_exp", "rt", "rank_p", "slot_p", "routed", "ohb_s"))
        val_s, passed = sem("val_s"), sem("passed")
        up_p, silu_s, hid_s, ht_p, hi_s, res_s, mid_s, lo_s, y_p, y_s = (sem("m_" + n) for n in (
            "up", "silu", "hid", "ht", "hi", "res", "mid", "lo", "y", "ys"))
        sh_s = sem("sh_s")
        ixg_s, ixp_s, rT_p, rT_s, yo_s = (sem(n) for n in ("ixg_s", "ixp_s", "rT_p", "rT_s", "yo_s"))
        fetch = [sem(f"fetch{k}") for k in range(RING)]
        put = [sem(f"put{k}") for k in range(RING)]
        ld_y = [sem(f"ld_y{k}") for k in range(B)]
        f_a, f_b, f_c, f_d = (sem("f_" + n) for n in "abcd")

        ld_cst, ld_x0, ld_x1, ld_w, ld_mod = (sem("ld_" + n) for n in ("cst", "x0", "x1", "w", "mod"))
        c_exp, c_den, c_inv, c_silu = (sem("c_" + n) for n in ("exp", "den", "inv", "silu"))
        mod_p, mod_r, g_sgn, g_abs, g_fin, modT_p, modT_s, mod_st, mod_ld = (sem(n) for n in (
            "mod_p", "mod_r", "g_sgn", "g_abs", "g_fin", "modT_p", "modT_s", "mod_st", "mod_ld"))
        pads, hw_s = sem("pads"), sem("hw_s")
        ln_st, ln_mv, ln_ve, ln_rs, ln_xn = (sem("ln_" + n) for n in ("st", "mv", "ve", "rs", "xn"))
        hT_p, hT_s, q_p, q_s, k_p, k_s, v_p, v_s = (sem(n) for n in (
            "hT_p", "hT_s", "q_p", "q_s", "k_p", "k_s", "v_p", "v_s"))
        s_p, s_m, st_p, s_mx, s_sub, s_ex, s_sum, s_ri, s_nm = (sem("s_" + n) for n in (
            "p", "m", "t", "mx", "sub", "ex", "sum", "ri", "nm"))
        pt_p, pt_s, z_p, z_s, o_s, pr_p, ga_s, x1_s = (sem(n) for n in (
            "pt_p", "pt_s", "z_p", "z_s", "o_s", "pr_p", "ga_s", "x1_s"))
        st_out = sem("st_out")

        block = ctx.enter_context(nc.Block())

        def wait(eng, s, v):
            if not (isinstance(v, int) and v <= 0):
                eng.wait_ge(s, v)

        def settle(eng):
            eng.sem_inc(passed, 1)

        def over(eng, main):
            main(0, True, 2)
            with eng.Fori(1, B - 2) as it:
                main(it, False, 2)
            main(B - 2, False, 1)
            main(B - 1, False, 0)

        def over_tiles(eng, step, n, k):
            for j in range(k):
                step(j, j, 0)
            with eng.Fori(1, n // k - 1) as i:
                for j in range(k):
                    step(k * i + j, j, i)
            for j in range(k):
                step(n - k + j, j, n // k - 1)

        def later(i, j, d):
            q, r = divmod(j + d, RING)
            return RING * (i + q) + r, r, i + q

        x_t = x.rearrange("(t p) d -> p t d", p=P)

        @block.sync
        def _(sp):
            sp.dma_start(xs[:, 0:U, :], x_t[:, 0:U, :]).then_inc(ld_x0, 16)
            sp.dma_start(cts[:, :, :], cT.rearrange("(c p) b -> p c b", p=P)).then_inc(ld_cst, 16)
            sp.dma_start(wms[:, :, :], wmod.rearrange("(c p) n -> p c n", p=P)).then_inc(ld_cst, 16)
            sp.dma_start(xs[:, U:TT, :], x_t[:, U:TT, :]).then_inc(ld_x1, 16)
            sp.wait_ge(g_fin, 1)
            sp.dma_start(moddram, modrow[:, :]).then_inc(mod_st, 16)
            sp.wait_ge(mod_st, 16)
            sp.dma_start(modb[:, :, :], moddram[:, 2 * D:6 * D].partition_broadcast(P)).then_inc(mod_ld, 16)
            hrows_t = hrows.rearrange("(b u p) k -> b p u k", u=U, p=P)
            def store_h(b):
                wait(sp, p_lo, b + 1)
                sp.dma_start(hrows_t[b], h3[:, :, :, :].rearrange("p u k d -> p u (k d)")).then_inc(st_h, 16)
            store_h(0)
            with sp.Fori(1, B) as b:
                store_h(b)
            sp.wait_ge(x1_s, TT)
            sp.dma_start(w13, w13T).then_inc(ld_ew, 16)
            sp.dma_start(w2, w2T).then_inc(ld_ew, 16)
            y_t = yrows.rearrange("(k b u p) d -> b p k u d", k=TOPK, u=U, p=P)
            sp.wait_ge(y_p, TT + NS)
            for k in range(RING):
                sp.wait_ge(put[k], 16 * (NS // RING))
            for b in range(B):
                for k in range(TOPK):
                    sp.dma_start(yk[:, k, U * b:U * b + U, :], y_t[b, :, k]).then_inc(ld_y[b], 16)
            out_t = out.rearrange("(b u p) d -> b p u d", u=U, p=P)
            for b in range(B):
                sp.wait_ge(f_d, b + 1)
                sp.dma_start(out_t[b], xs[:, U * b:U * b + U, :]).then_inc(st_out, 16)
            sp.wait_ge(st_out, 16 * B)

        @block.gpsimd
        def _(gp):
            gp.memset(ones_row[:, :], 1.0)
            gp.memset(ohb[:, TT, :], 0.0)
            gp.memset(hid[:, :, :], 0.0)
            gp.memset(hT[:, :, :], 0.0)
            gp.memset(kT[:, :, :], 0.0).then_inc(pads, 1)
            gp.wait_ge(ld_w, 80)

            def rstd1(b):
                wait(gp, ln_ve, b + 1)
                gp.tensor_tensor(rstd[:, :], ve[:, :], nhalf, ALU.pow).then_inc(ln_rs, 1)

            def rstd2(b):
                wait(gp, l2_ve, b + 1)
                gp.tensor_tensor(rstd2s[:, :], ve2[:, :], nhalf, ALU.pow).then_inc(l2_rs, 1)

            def split(b):
                wait(gp, l2_xn, b + 1)
                gp.tensor_tensor(h2[:, :, :], h2[:, :, :],
                                 modb[:, b, 2 * D:3 * D].unsqueeze(1).to_broadcast([P, U, D]), ALU.mult).then_inc(l2_mu, 1)
                wait(gp, l2_mu, b + 1)
                gp.tensor_tensor(h2[:, :, :], h2[:, :, :],
                                 modb[:, b, D:2 * D].unsqueeze(1).to_broadcast([P, U, D]), ALU.add).then_inc(l2_h, 1)
                wait(gp, p_hi, b + 1)
                gp.tensor_tensor(hr[:, :, :], h2[:, :, :], h3[:, :, 0], ALU.subtract).then_inc(p_r, 1)
                wait(gp, p_mid, b + 1)
                gp.tensor_tensor(h3[:, :, 2], hr[:, :, :], h3[:, :, 1], ALU.subtract).then_inc(p_lo, 1)

            def main(it, first, after):
                if first:
                    gp.wait_ge(mod_ld, 16)
                else:
                    split(it - 1)
                if after > 1:
                    rstd1(it + 2)
                rstd2(it)

            rstd1(0)
            rstd1(1)
            over(gp, main)
            split(B - 1)

            def lo(n, w, j):
                p, k = w
                wait(gp, mid_s, n + 1)
                wait(gp, y_p, n - 1)
                gp.tensor_tensor(hT3[0:p, j % 2, 2, 0:k], hres[0:p, j % 2, 0:k], hT3[0:p, j % 2, 1, 0:k],
                                 ALU.subtract).then_inc(lo_s, 1)

            over_tiles(gp, lambda t, j, i: lo(t, SHARED_W, j), TT, 2)

            gp.wait_ge(st_h, 16 * B)
            gp.wait_ge(routed, 1)

            def get(s, j, i):
                wait(gp, rT_p, s - RING + 1)
                settle(gp)
                gp.tensor_copy(ixg[:, j:j + 1], sloti[:, 0, bass.ds(s, 1)]).then_inc(ixg_s, 1)
                wait(gp, ixg_s, s + 1)
                settle(gp)
                gp.indirect_dma_start(rows[:, j, :], None, hrows,
                                      bass.IndirectOffsetOnAxis(ap=ixg[:, j:j + 1], axis=0)).then_inc(fetch[j], 16)

            def give(s, j, i):
                wait(gp, put[j], 16 * i)
                settle(gp)
                gp.tensor_copy(ixp[:, j:j + 1], sloti[:, 1, bass.ds(s, 1)]).then_inc(ixp_s, 1)
                wait(gp, yo_s, s + 1)
                wait(gp, ixp_s, s + 1)
                settle(gp)
                gp.indirect_dma_start(yrows, bass.IndirectOffsetOnAxis(ap=ixp[:, j:j + 1], axis=0),
                                      yo[:, j, :], None, bounds_check=TOPK * T - 1,
                                      oob_is_err=False).then_inc(put[j], 16)

            def step(s, j, i):
                if not (isinstance(s, int) and s + AHEAD >= NS):
                    get(*later(i, j, AHEAD))
                lo(TT + s, EXPERT_W, j)
                if not (isinstance(s, int) and s == 0):
                    give(*later(i, j, -1))

            for s in range(AHEAD):
                get(s, s, 0)
            over_tiles(gp, step, NS, RING)
            give(NS - 1, RING - 1, NS // RING - 1)

            for b in range(B):
                gp.wait_ge(f_b, b + 1)
                v = yk[:, 0, U * b:U * b + U, :]
                gp.tensor_tensor(v, v, modb[:, b, 3 * D:].unsqueeze(1).to_broadcast([P, U, D]),
                                 ALU.mult).then_inc(f_c, 1)

        @block.scalar
        def _(act):
            act.dma_start(cft[:, :], cf).then_inc(ld_w, 16)
            act.dma_start(cbt[:, :], cb).then_inc(ld_w, 16)
            act.dma_start(wqkv[:, :, :], wqkvT.rearrange("(c p) n -> p c n", p=P)).then_inc(ld_w, 16)
            act.dma_start(wpj[:, :, :], projT.rearrange("(c p) n -> p c n", p=P)).then_inc(ld_w, 16)
            act.dma_start(pb[:, :], proj_b).then_inc(ld_w, 16)
            act.dma_start(gws[:, :, :], gateT.rearrange("(c p) e -> p c e", p=P)).then_inc(ld_g, 16)
            act.dma_start(sw13[:, :, :], sw13T).then_inc(ld_sw, 16)
            act.dma_start(sw2[:, :, :], sw2T).then_inc(ld_sw, 16)
            act.wait_ge(ld_cst, 32)
            act.activation(csig[:, :, :], cts[:, :, :], ACT.Exp, scale=-1.0).then_inc(c_exp, 1)

            def scaled_h(b):
                wait(act, hT_p, b + 1)
                if isinstance(b, int) and b == 0:
                    act.wait_ge(pads, 1)
                    act.wait_ge(modT_s, 1)
                wait(act, k_p, b)
                wait(act, hw_s, b)
                for c in range(C):
                    last = act.activation(hT[:, c, WIN:WIN + N], M0[:, c * N:(c + 1) * N], ACT.Identity,
                                          scale=modT[:, 2 + c, bass.ds(b, 1)], bias=modT[:, c, bass.ds(b, 1)])
                last.then_inc(hT_s, 1)

            def spread_q(b, c):
                if c == 0:
                    wait(act, q_p, b + 1)
                    wait(act, s_p, U * b)
                for h in range(GH):
                    last = act.activation(qbd[:, c, :, h], M1[:, c * N:(c + 1) * N], ACT.Copy,
                                          scale=headsel[:, h:h + 1])
                if c == C - 1:
                    last.then_inc(q_s, 1)

            def keep_k(b):
                wait(act, k_p, b + 1)
                for c in range(C):
                    last = act.activation(kT[:, c, WIN:WIN + N], M0[:, c * N:(c + 1) * N], ACT.Copy)
                last.then_inc(k_s, 1)

            def keep_v(b):
                wait(act, v_p, b + 1)
                wait(act, z_p, NQ * U * b)
                act.activation(vw[:, :, :], bank[3][:, :], ACT.Copy).then_inc(v_s, 1)

            def turned_p(it, u):
                n = U * it + u
                wait(act, pt_p, n + 1)
                wait(act, z_p, NQ * (n - U + 1))
                act.activation(PT[:, u], SP[u][:, :], ACT.Copy).then_inc(pt_s, 1)

            def first_parts(b):
                wait(act, l2_h, b + 1)
                act.activation(h3[:, :, 0], h2[:, :, :], ACT.Copy).then_inc(p_hi, 1)
                wait(act, p_r, b + 1)
                act.activation(h3[:, :, 1], hr[:, :, :], ACT.Copy).then_inc(p_mid, 1)

            def turned_parts(b):
                wait(act, xT_p, b + 1)
                for u in range(U):
                    last = act.activation(xT[:, U * b + u].rearrange("p q t -> p (q t)"), MB[u], ACT.Copy)
                last.then_inc(xT_s, 1)

            def main(it, first, after):
                if after:
                    scaled_h(it + 1)
                if not first:
                    first_parts(it - 1)
                for u in range(U):
                    n = U * it + u
                    wait(act, s_sub, n + 1)
                    act.activation(S[:, u], S[:, u], ACT.Exp).then_inc(s_ex, 1)
                if not first:
                    turned_parts(it - 1)
                if after:
                    spread_q(it + 1, 0)
                turned_p(it, 0)
                turned_p(it, 1)
                if after:
                    spread_q(it + 1, 1)
                    keep_k(it + 1)
                if not first:
                    wait(act, st_h, 16 * it)
                if after:
                    keep_v(it + 1)

            scaled_h(0)
            spread_q(0, 0)
            spread_q(0, 1)
            keep_k(0)
            keep_v(0)
            over(act, main)
            first_parts(B - 1)
            turned_parts(B - 1)

            act.wait_ge(lg_s, B)
            act.activation(score[:, :, :], logit[:, :, :], ACT.Exp, scale=-1.0).then_inc(r_exp, 1)

            def silu(n, w, j):
                wait(act, up_p, n + 1)
                wait(act, hid_s, n - 1)
                act.activation(act_s[:, j % 2, 0:w], bank[j % 2][:, 0:w], ACT.Silu).then_inc(silu_s, 1)

            def hi(n, w, j):
                p, k = w
                wait(act, ht_p, n + 1)
                wait(act, y_p, n - 1)
                act.activation(hT3[0:p, j % 2, 0, 0:k], HT(j)[0:p, 0:k], ACT.Copy).then_inc(hi_s, 1)

            def mid(n, w, j):
                p, k = w
                wait(act, res_s, n + 1)
                act.activation(hT3[0:p, j % 2, 1, 0:k], hres[0:p, j % 2, 0:k], ACT.Copy).then_inc(mid_s, 1)

            def shared(t, j, i):
                hi(t, SHARED_W, j)
                if not (isinstance(t, int) and t + 1 == TT):
                    silu(t + 1, SI, j + 1)
                mid(t, SHARED_W, j)

            silu(0, SI, 0)
            over_tiles(act, shared, TT, 2)

            def result(s, j, i):
                wait(act, y_p, TT + s + 1)
                wait(act, put[j], 16 * i)
                if isinstance(s, int) and s == 0:
                    act.wait_ge(sh_s, TT)
                act.activation(yo[:, j, :], YP(j), ACT.Copy).then_inc(yo_s, 1)

            def step(s, j, i):
                hi(TT + s, EXPERT_W, j)
                if not (isinstance(s, int) and s + 1 == NS):
                    silu(TT + s + 1, I, j + 1)
                mid(TT + s, EXPERT_W, j)
                if not (isinstance(s, int) and s == 0):
                    result(*later(i, j, -1))

            silu(TT, I, 0)
            over_tiles(act, step, NS, RING)
            result(NS - 1, RING - 1, NS // RING - 1)

            for b in range(B):
                act.wait_ge(ld_y[b], 16 * TOPK)
                for u in range(U):
                    last = act.activation(yk[:, 0, U * b + u], yk[:, 0, U * b + u], ACT.Copy,
                                          scale=gatew[:, 0, U * b + u:U * b + u + 1])
                last.then_inc(f_a, 1)

        @block.vector
        def _(dve):
            dve.wait_ge(c_exp, 1)
            dve.tensor_scalar(csig[:, :, :], csig[:, :, :], 1.0, None, ALU.add).then_inc(c_den, 1)
            dve.wait_ge(c_den, 1)
            dve.reciprocal(csig[:, :, :], csig[:, :, :]).then_inc(c_inv, 1)
            dve.wait_ge(c_inv, 1)
            dve.tensor_tensor(cts[:, :, :], cts[:, :, :], csig[:, :, :], ALU.mult).then_inc(c_silu, 1)
            dve.wait_ge(mod_p, 1)
            dve.tensor_copy(modrow[:, 0:4 * D], bank[0][0:B, 0:1024])
            dve.tensor_copy(modrow[:, 4 * D:6 * D], bank[1][0:B, 0:512]).then_inc(mod_r, 1)
            dve.wait_ge(mod_r, 1)
            for k in (1, 4):
                dve.tensor_scalar(modrow[:, k * D:(k + 1) * D], modrow[:, k * D:(k + 1) * D], 1.0, None, ALU.add)
            for i, k in enumerate((2, 5)):
                g = modrow[:, k * D:(k + 1) * D]
                dve.tensor_scalar(gtmp[:, i], g, 0.0, 2.0, ALU.is_ge, ALU.mult)
                last = dve.scalar_tensor_tensor(gtmp[:, 2 + i], g, -1.0, g, ALU.mult, ALU.max)
            last.then_inc(g_sgn, 1)
            dve.wait_ge(g_sgn, 1)
            dve.tensor_scalar(gtmp[:, 0:2], gtmp[:, 0:2], -1.0, None, ALU.add)
            dve.tensor_scalar(gtmp[:, 2:4], gtmp[:, 2:4], 0.25, None, ALU.max).then_inc(g_abs, 1)
            dve.wait_ge(g_abs, 1)
            for i, k in enumerate((2, 5)):
                last = dve.tensor_tensor(modrow[:, k * D:(k + 1) * D], gtmp[:, i], gtmp[:, 2 + i], ALU.mult)
            last.then_inc(g_fin, 1)
            dve.wait_ge(modT_p, 1)
            dve.tensor_copy(modT[:, :, :], M0[:, 0:4 * B]).then_inc(modT_s, 1)

            def stats(xt, k):
                for u in range(U):
                    last = dve.bn_stats(bst[:, u], xt(u))
                last.then_inc(ln_st, 1)
                wait(dve, ln_st, k)
                settle(dve)
                for u in range(U):
                    last = dve.bn_aggr(mv[:, u], bst[:, u])
                last.then_inc(ln_mv, 1)
                wait(dve, ln_mv, k)
                dve.tensor_scalar(ve[:, :], mv[:, :, 1], EPS, None, ALU.add).then_inc(ln_ve, 1)

            def ln1_stats(b):
                stats(lambda u: xs[:, U * b + u, :], b + 1)

            def ln1_apply(b):
                wait(dve, ln_rs, b + 1)
                wait(dve, hT_p, b)
                for u in range(U):
                    last = dve.tensor_scalar(xn[:, u], xs[:, U * b + u, :], mv[:, u, 0:1], rstd[:, u:u + 1],
                                             ALU.subtract, ALU.mult)
                last.then_inc(ln_xn, 1)

            def key_windows(b):
                wait(dve, hT_s, b + 1)
                wait(dve, v_p, b)
                settle(dve)
                for c in range(C):
                    a = hT[:, c, :]
                    last = dve.tensor_copy(hw[:, c], bass.AP(a.tensor, a.offset, [a.ap[0], [QB, N // QB], [1, KB]]))
                last.then_inc(hw_s, 1)

            def logits(b):
                wait(dve, lg_p, b + 1)
                for u in range(U):
                    last = dve.tensor_reduce(logit[:, U * b + u, :], LG[u].rearrange("p (k e) -> p e k", e=E),
                                             AX.X, ALU.add)
                last.then_inc(lg_s, 1)

            def own_heads(it, k):
                if k < NQ * U:
                    u, r = divmod(k, NQ)
                    n = U * it + u
                    wait(dve, z_p, NQ * U * it + k + 1)
                    dve.tensor_tensor(Z[:, r], ZP[:, (r % 2) * 512:(r % 2 + 1) * 512].rearrange("p (k h) -> p k h", h=GH),
                                      headsel.unsqueeze(1).to_broadcast([P, 512 // GH, GH]), ALU.mult).then_inc(z_s, 1)
                if k > 0:
                    u, r = divmod(k - 1, NQ)
                    n = U * it + u
                    wait(dve, z_s, NQ * U * it + k)
                    if r == 0:
                        wait(dve, pr_p, n - U + 1)
                    ov = OT[:, u].rearrange("p c (q r t) -> p r q c t", q=2, r=BPT)
                    last = dve.tensor_reduce(ov[:, r], Z[:, r].rearrange("p (q c t) h -> p q c t h", q=2, c=C),
                                             AX.X, ALU.add)
                    if r == NQ - 1:
                        last.then_inc(o_s, 1)

            def main(it, first, after):
                for u in range(U):
                    n = U * it + u
                    wait(dve, s_p, n + 1)
                    wait(dve, st_p, n - U + 1)
                    dve.tensor_tensor(ST[:, u], SP[u][:, :].rearrange("p (k j) -> p k j", j=P),
                                      window.unsqueeze(1).to_broadcast([P, NBLK // BPT, P]),
                                      ALU.mult).then_inc(s_m, 1)
                for u in range(U):
                    n = U * it + u
                    wait(dve, st_p, n + 1)
                    sv = SP[u][:, :].rearrange("p (k j) -> p k j", j=KB)
                    dve.tensor_reduce(mx[:, u], sv, AX.X, ALU.max).then_inc(s_mx, 1)
                    wait(dve, s_mx, n + 1)
                    wait(dve, pt_p, n - U + 1)
                    dve.tensor_tensor(S[:, u], sv, mx[:, u, :].unsqueeze(2).to_broadcast([P, NBLK, KB]),
                                      ALU.subtract).then_inc(s_sub, 1)
                for u in range(U):
                    n = U * it + u
                    wait(dve, s_ex, n + 1)
                    dve.tensor_reduce(rs[:, u], S[:, u], AX.X, ALU.add).then_inc(s_sum, 1)
                    wait(dve, s_sum, n + 1)
                    dve.reciprocal(ri[:, u], rs[:, u]).then_inc(s_ri, 1)
                    wait(dve, s_ri, n + 1)
                    dve.tensor_tensor(S[:, u], S[:, u], ri[:, u, :].unsqueeze(2).to_broadcast([P, NBLK, KB]),
                                      ALU.mult).then_inc(s_nm, 1)
                if after > 1:
                    ln1_stats(it + 2)
                if after:
                    key_windows(it + 1)
                if not first:
                    logits(it - 1)
                if after > 1:
                    ln1_apply(it + 2)
                for k in range(NQ * U + 1):
                    own_heads(it, k)
                if first:
                    dve.wait_ge(mod_ld, 16)
                for u in range(U):
                    n = U * it + u
                    wait(dve, pr_p, n + 1)
                    dve.tensor_tensor(ao[:, u], SP[u][:, 512:512 + D], modb[:, it, 0:D], ALU.mult).then_inc(ga_s, 1)
                    wait(dve, ga_s, n + 1)
                    dve.tensor_tensor(xs[:, n, :], xs[:, n, :], ao[:, u], ALU.add).then_inc(x1_s, 1)
                wait(dve, x1_s, U * it + U)
                settle(dve)
                for u in range(U):
                    last = dve.bn_stats(bst2[:, u], xs[:, U * it + u, :])
                last.then_inc(l2_st, 1)
                wait(dve, l2_st, it + 1)
                settle(dve)
                for u in range(U):
                    last = dve.bn_aggr(mv2[:, u], bst2[:, u])
                last.then_inc(l2_mv, 1)
                wait(dve, l2_mv, it + 1)
                dve.tensor_scalar(ve2[:, :], mv2[:, :, 1], EPS, None, ALU.add).then_inc(l2_ve, 1)
                wait(dve, l2_rs, it + 1)
                wait(dve, p_r, it)
                for u in range(U):
                    last = dve.tensor_scalar(h2[:, u], xs[:, U * it + u, :], mv2[:, u, 0:1], rstd2s[:, u:u + 1],
                                             ALU.subtract, ALU.mult)
                last.then_inc(l2_xn, 1)

            dve.wait_ge(ld_x0, 16)
            ln1_stats(0)
            ln1_apply(0)
            key_windows(0)
            dve.wait_ge(ld_x1, 16)
            ln1_stats(1)
            ln1_apply(1)
            dve.wait_ge(ld_g, 16)
            for k in range(PARTS):
                dve.tensor_copy(gw3[:, :, k, :], gws[:, :, :]).then_inc(gw_s, 1)
                if k < PARTS - 1:
                    dve.wait_ge(gw_s, 2 * k + 1)
                    dve.tensor_tensor(gws[:, :, :], gws[:, :, :], gw3[:, :, k, :], ALU.subtract).then_inc(gw_s, 1)
                    dve.wait_ge(gw_s, 2 * k + 2)
            over(dve, main)
            logits(B - 1)

            links = [0]

            def link(ins):
                links[0] += 1
                ins.then_inc(rt, 1)
                dve.wait_ge(rt, links[0])

            dve.wait_ge(r_exp, 1)
            link(dve.tensor_scalar(score[:, :, :], score[:, :, :], 1.0, None, ALU.add))
            link(dve.reciprocal(score[:, :, :], score[:, :, :]))
            revb = rev.unsqueeze(1).to_broadcast([P, TT, E])
            for k in range(TOPK):
                link(dve.tensor_reduce(top[:, k], score[:, :, :], AX.X, ALU.max))
                link(dve.tensor_tensor(cand[:, :, :], score[:, :, :],
                                       top[:, k].unsqueeze(2).to_broadcast([P, TT, E]), ALU.is_equal))
                link(dve.tensor_tensor(cand[:, :, :], cand[:, :, :], revb, ALU.mult))
                link(dve.tensor_reduce(rtop[:, k], cand[:, :, :], AX.X, ALU.max))
                link(dve.tensor_tensor(oh[:, k], rtop[:, k].unsqueeze(2).to_broadcast([P, TT, E]), revb,
                                       ALU.is_equal))
                if k == 0:
                    link(dve.scalar_tensor_tensor(score[:, :, :], oh[:, k], -2.0, score[:, :, :],
                                                  ALU.mult, ALU.add))
            dve.tensor_tensor(ohb[:, 0:TT, :], oh[:, 0], oh[:, 1], ALU.add).then_inc(ohb_s, 1)
            link(dve.tensor_tensor(den[:, :], top[:, 0], top[:, 1], ALU.add))
            link(dve.reciprocal(den[:, :], den[:, :]))
            dve.tensor_tensor(gatew[:, :, :], top[:, :, :], den[:, :].unsqueeze(1).to_broadcast([P, TOPK, TT]),
                              ALU.mult)
            dve.wait_ge(rank_p, 1)
            rank = bank[0][:, 0:TT * E].rearrange("p (t e) -> p t e", e=E)
            link(dve.tensor_scalar(cnti[:, :], bank[0][:, TT * E:TT * E + E], float(P - 1), None, ALU.add))
            link(dve.tensor_scalar(cnti[:, :], cnti[:, :], P.bit_length() - 1, None, ALU.arith_shift_right))
            link(dve.tensor_copy(cnt[:, 0], cnti[:, :]))
            link(dve.tensor_tensor_scan(cnt[:, 1], one, cnt[:, 0], 0.0, ALU.mult, ALU.add))
            link(dve.tensor_tensor(cnt[:, 2], cnt[:, 1], cnt[:, 0], ALU.subtract))
            link(dve.tensor_scalar(cnt[:, 3], cnt[:, 2], float(P), None, ALU.mult))
            link(dve.tensor_tensor(cand[:, :, :], rank, cnt[:, 3].unsqueeze(1).to_broadcast([P, TT, E]), ALU.add))
            for k in range(TOPK):
                link(dve.tensor_tensor(oh[:, k], oh[:, k], cand[:, :, :], ALU.mult))
            link(dve.tensor_reduce(pos[:, :], oh[:, :, :, :].rearrange("p k t e -> p (k t) e"), AX.X, ALU.add))
            link(dve.tensor_copy(posi[:, 0], pos[:, :]))
            link(dve.tensor_scalar(posi[:, 1], posi[:, 0], P - 1, None, ALU.bitwise_and))
            link(dve.tensor_scalar(posi[:, 2], posi[:, 0], P.bit_length() - 1, None, ALU.arith_shift_right))
            link(dve.tensor_copy(posf[:, :, :], posi[:, 1:3]))
            TK = TOPK * TT
            dve.tensor_tensor(lane_oh[:, :, :], lane.unsqueeze(1).to_broadcast([P, TK, P]),
                              posf[:, 0].unsqueeze(2).to_broadcast([P, TK, P]), ALU.is_equal)
            link(dve.tensor_tensor(tile_oh[:, :, :], tileno.unsqueeze(1).to_broadcast([P, TK, NS]),
                                   posf[:, 1].unsqueeze(2).to_broadcast([P, TK, NS]), ALU.is_equal))
            dve.tensor_tensor(val[:, :, 0], tile_oh[:, :, :], turn.unsqueeze(2).to_broadcast([P, TK, NS]), ALU.mult)
            dve.tensor_scalar(val[:, :, 1], tile_oh[:, :, :], row1, None, ALU.mult).then_inc(val_s, 1)
            link(dve.tensor_tensor(owner[:, :, :], tileno.unsqueeze(2).to_broadcast([P, NS, E]),
                                   cnt[:, 1].unsqueeze(1).to_broadcast([P, NS, E]), ALU.is_ge))
            link(dve.tensor_reduce(slot[:, 0], owner[:, :, :], AX.X, ALU.add))
            link(dve.tensor_scalar(expert[:, :], slot[:, 0], float(E - 1), None, ALU.min))
            dve.wait_ge(slot_p, 1)
            who = bank[1][:, 0:2 * NS].rearrange("p (k s) -> p k s", k=2)
            link(dve.tensor_copy(slot[:, 0:2], who))
            link(dve.scalar_tensor_tensor(slot[:, 2], slot[:, 0], float(P), slot[:, 1], ALU.mult, ALU.add))
            link(dve.tensor_scalar(slot[:, 3], slot[:, 1], 0.0, float(NONE), ALU.is_equal, ALU.mult))
            dve.tensor_scalar(sloti[:, 0], slot[:, 2], -1.0, 0.0, ALU.add, ALU.max)
            link(dve.scalar_tensor_tensor(sloti[:, 1], slot[:, 2], -1.0, slot[:, 3], ALU.add, ALU.add))
            dve.tensor_scalar(sloti[:, 0], sloti[:, 0], T - 1, None, ALU.bitwise_and).then_inc(routed, 1)

            def hidden(n, w, boff, j):
                wait(dve, silu_s, n + 1)
                wait(dve, ht_p, n - 1)
                dve.tensor_tensor(hid[:, j % 2, 0:w], act_s[:, j % 2, 0:w], bank[j % 2][:, boff:boff + w],
                                  ALU.mult).then_inc(hid_s, 1)

            def rest(n, w, j):
                p, k = w
                wait(dve, hi_s, n + 1)
                wait(dve, lo_s, n - 1)
                dve.tensor_tensor(hres[0:p, j % 2, 0:k], HT(j)[0:p, 0:k], hT3[0:p, j % 2, 0, 0:k],
                                  ALU.subtract).then_inc(res_s, 1)

            def base(t, j, b):
                wait(dve, y_p, t + 1)
                dve.tensor_tensor(yo[:, j, :], YP(j), modb[:, b, 3 * D:], ALU.mult).then_inc(y_s, 1)
                wait(dve, y_s, t + 1)
                dve.tensor_tensor(xs[:, t, :], xs[:, t, :], yo[:, j, :], ALU.add).then_inc(sh_s, 1)

            def shared(t, j, i):
                if not (isinstance(t, int) and t + 1 == TT):
                    hidden(t + 1, SI, 512, j + 1)
                rest(t, SHARED_W, j)
                if not (isinstance(t, int) and t == 0):
                    base(t - 1, 1 - j, i if j == 1 else i - 1)

            hidden(0, SI, 512, 0)
            over_tiles(dve, shared, TT, 2)
            base(TT - 1, 1, B - 1)

            def rows_turned(s, j, i):
                wait(dve, rT_p, s + 1)
                wait(dve, up_p, TT + s - 1)
                dve.tensor_copy(rT[:, j % 2].rearrange("p q t -> p (q t)"), RTP(j)).then_inc(rT_s, 1)

            def step(s, j, i):
                if not (isinstance(s, int) and s + 1 == NS):
                    hidden(TT + s + 1, I, I, j + 1)
                rest(TT + s, EXPERT_W, j)
                if not (isinstance(s, int) and s + 2 >= NS):
                    rows_turned(*later(i, j, 2))

            def finish(b):
                dve.wait_ge(f_c, b + 1)
                v = xs[:, U * b:U * b + U, :]
                dve.tensor_tensor(v, v, yk[:, 0, U * b:U * b + U, :], ALU.add).then_inc(f_d, 1)

            rows_turned(0, 0, 0)
            hidden(TT, I, I, 0)
            rows_turned(1, 1, 0)
            over_tiles(dve, step, NS, RING)

            for b in range(B):
                dve.wait_ge(f_a, b + 1)
                for u in range(U):
                    k = U * b + u
                    last = dve.scalar_tensor_tensor(yk[:, 0, k], yk[:, 1, k], gatew[:, 1, k:k + 1], yk[:, 0, k],
                                                    ALU.mult, ALU.add)
                last.then_inc(f_b, 1)
                if b:
                    finish(b - 1)
            finish(B - 1)

        @block.tensor
        def _(pe):
            pe.wait_ge(c_silu, 1)
            for j in range(3):
                o = bank[j // 2][0:B, (j % 2) * 512:(j % 2 + 1) * 512]
                for c in range(C):
                    last = pe.matmul(o, cts[:, c, :], wms[:, c, j * 512:(j + 1) * 512], start=c == 0, stop=c == C - 1)
            last.then_inc(mod_p, 1)
            pe.wait_ge(ld_w, 80)
            pe.wait_ge(g_fin, 1)
            for k in range(4):
                last = pe.transpose(M0[:, k * B:(k + 1) * B], modrow[:, k * P:(k + 1) * P], ident[0:B, 0:B])
            last.then_inc(modT_p, 1)

            def turn_x(b):
                wait(pe, ln_xn, b + 1)
                wait(pe, v_s, b)
                if isinstance(b, int) and b == 0:
                    pe.wait_ge(modT_s, 1)
                for c in range(C):
                    for u in range(U):
                        last = pe.transpose(M0[:, c * N + u * P:c * N + (u + 1) * P],
                                            xn[:, u, c * P:(c + 1) * P], ident)
                last.then_inc(hT_p, 1)

            def product(bank_half, off, done):
                for c in range(C):
                    for k in range(C):
                        last = pe.matmul(bank_half[:, c * N:(c + 1) * N], wqkv[:, k, off + c * P:off + (c + 1) * P],
                                         hT[:, k, WIN:WIN + N], start=k == 0, stop=k == C - 1)
                last.then_inc(done, 1)

            def make_q(b):
                wait(pe, hT_s, b + 1)
                product(M1, 0, q_p)

            def make_k(b):
                product(M0, D, k_p)

            def make_v(b, part):
                if part == 0:
                    wait(pe, hw_s, b + 1)
                    wait(pe, k_s, b + 1)
                    wait(pe, q_s, b + 1)
                for w in range(2 * part, 2 * part + 2):
                    for k in range(C):
                        last = pe.matmul(bank[3][:, w * D:(w + 1) * D], hw[:, k, BPT * w:BPT * (w + 1), :],
                                         wqkv[:, k, 2 * D:3 * D], start=k == 0, stop=k == C - 1)
                if part == 1:
                    last.then_inc(v_p, 1)

            def scores(it, u):
                n = U * it + u
                wait(pe, q_s, it + 1)
                wait(pe, k_s, it + 1)
                wait(pe, ga_s, n - U + 1)
                for s in range(2):
                    pe.matmul(SP[u][:, s * 512:(s + 1) * 512], identb, addmask(u), start=True, stop=False,
                              skip_group_check=True)
                for c in range(C):
                    for b in range(BL):
                        for s in range(2):
                            q0 = u * P + b * QB
                            r, o = b % BPT, ((s * C + c) * 2 + b // BPT) * P
                            last = pe.matmul(SP[u][KB * r:KB * (r + 1), o:o + P],
                                             kT[GC * s:GC * (s + 1), c, q0:q0 + KB],
                                             qbd[GC * s:GC * (s + 1), c, q0:q0 + QB, :],
                                             start=False, stop=True, skip_group_check=True)
                last.then_inc(s_p, 1)

            def turn_s(it, u):
                wait(pe, s_m, U * it + u + 1)
                for j in range(NBLK // BPT):
                    last = pe.transpose(SP[u][:, j * P:(j + 1) * P], ST[:, u, j, :], ident)
                last.then_inc(st_p, 1)

            def turn_p(it, u):
                wait(pe, s_nm, U * it + u + 1)
                for j in range(NBLK // BPT):
                    last = pe.transpose(SP[u][:, j * P:(j + 1) * P], S[:, u, BPT * j:BPT * (j + 1), :], ident)
                last.then_inc(pt_p, 1)

            def times_v(it, k):
                u, r = divmod(k, NQ)
                if k == 0:
                    wait(pe, v_s, it + 1)
                    wait(pe, lg_s, it)
                if r == 0:
                    wait(pe, pt_s, U * it + u + 1)
                wait(pe, z_s, NQ * U * it + k - 1)
                for q in range(2):
                    for c in range(C):
                        for s in range(2):
                            g, o = 2 * c + s, (r % 2) * 512 + (q * C + c) * P
                            last = pe.matmul(ZP[GC * s:GC * (s + 1), o:o + P],
                                             vw[KB * r:KB * (r + 1), 2 * u + q, g * GC:(g + 1) * GC],
                                             PT[KB * r:KB * (r + 1), u, (s * C + c) * 2 + q, :],
                                             start=True, stop=True, skip_group_check=True)
                last.then_inc(z_p, 1)

            def project(it, u):
                n = U * it + u
                wait(pe, o_s, n + 1)
                o = SP[u][:, 512:512 + D]
                pe.matmul(o, ones_row[:, :], pb[:, :], start=True, stop=False)
                for c in range(C):
                    last = pe.matmul(o, OT[:, u, c, :], wpj[:, c, :], start=False, stop=c == C - 1)
                last.then_inc(pr_p, 1)

            def turn_parts(b):
                wait(pe, p_lo, b + 1)
                wait(pe, z_s, NQ * U * (b + 1))
                for u in range(U):
                    for q in range(PARTS * C):
                        last = pe.transpose(MB[u][:, q * P:(q + 1) * P],
                                            h3[:, u, q // C, (q % C) * P:(q % C + 1) * P], identb)
                last.then_inc(xT_p, 1)

            def gate(b):
                wait(pe, xT_s, b + 1)
                for u in range(U):
                    for q in range(PARTS * C):
                        last = pe.matmul(LG[u], xT[:, U * b + u, q, :], gw3[:, q % C].rearrange("p k e -> p (k e)"),
                                         start=q == 0, stop=q == PARTS * C - 1)
                last.then_inc(lg_p, 1)

            def main(it, first, after):
                scores(it, 0)
                scores(it, 1)
                if after:
                    turn_x(it + 1)
                turn_s(it, 0)
                turn_s(it, 1)
                if after:
                    make_q(it + 1)
                if not first:
                    turn_parts(it - 1)
                if after:
                    make_k(it + 1)
                turn_p(it, 0)
                if not first:
                    gate(it - 1)
                turn_p(it, 1)
                for k in range(NQ * U):
                    times_v(it, k)
                    if k == NQ + 1:
                        project(it, 0)
                if after:
                    make_v(it + 1, 0)
                project(it, 1)
                if after:
                    make_v(it + 1, 1)

            turn_x(0)
            make_q(0)
            make_k(0)
            make_v(0, 0)
            make_v(0, 1)
            over(pe, main)
            turn_parts(B - 1)
            gate(B - 1)

            pe.wait_ge(ohb_s, 1)
            pe.matmul(bank[0][:, 0:(TT + 1) * E], before, ohb[:, :, :].rearrange("p t e -> p (t e)"), start=True, stop=False,
                      skip_group_check=True)
            for t in range(TT):
                last = pe.matmul(bank[0][:, (t + 1) * E:(TT + 1) * E].rearrange("p (t e) -> p t e", e=E), onesb,
                                 ohb[:, t, :].unsqueeze(1).to_broadcast([P, TT - t, E]), start=False, stop=t == TT - 1,
                                 skip_group_check=True)
            last.then_inc(rank_p, 1)
            pe.wait_ge(val_s, 1)
            for k in range(TOPK * TT):
                last = pe.matmul(bank[1][:, 0:2 * NS], lane_oh[:, k, :], val[:, k].rearrange("p v s -> p (v s)"),
                                 start=k == 0, stop=k == TOPK * TT - 1)
            last.then_inc(slot_p, 1)

            def turn_hidden(n, k, p, j):
                wait(pe, hid_s, n + 1)
                wait(pe, res_s, n - 1)
                for q in range(k):
                    last = pe.transpose(HT(j)[0:p, q, :], hid[:, j % 2, q * p:(q + 1) * p], ident)
                last.then_inc(ht_p, 1)

            def up_shared(t, j):
                wait(pe, hid_s, t - 1)
                for half in range(2):
                    for q in range(PARTS * C):
                        last = pe.matmul(bank[j % 2][:, half * 512:half * 512 + SI], xT[:, t, q, :],
                                         sw13[:, q % C, half * SI:(half + 1) * SI],
                                         start=q == 0, stop=q == PARTS * C - 1)
                last.then_inc(up_p, 1)

            def down_shared(t, j):
                wait(pe, lo_s, t + 1)
                wait(pe, y_s, t - 1)
                last_k = SI - (SK - 1) * P
                for k in range(SK):
                    p = P if k < SK - 1 else last_k
                    for q in range(PARTS):
                        last = pe.matmul(YP(j), hT3[0:p, j % 2, q, k, :], sw2[0:p, k, :],
                                         start=k == 0 and q == 0, stop=k == SK - 1 and q == PARTS - 1)
                last.then_inc(y_p, 1)

            def shared(t, j, i):
                turn_hidden(t, SK, P, j)
                if not (isinstance(t, int) and t + 1 == TT):
                    up_shared(t + 1, j + 1)
                if not (isinstance(t, int) and t == 0):
                    down_shared(t - 1, j + 1)

            pe.wait_ge(routed, 1)
            pe.wait_ge(ld_sw, 32)
            up_shared(0, 0)
            over_tiles(pe, shared, TT, 2)
            down_shared(TT - 1, 1)

            def turn_rows(s, j, i):
                wait(pe, fetch[j], 16 * (i + 1))
                wait(pe, rT_s, s - 1)
                if isinstance(s, int) and s < 2:
                    pe.wait_ge(hid_s, TT)
                for q in range(PARTS * C):
                    last = pe.transpose(RTP(j)[:, q * P:(q + 1) * P], rows[:, j, q * P:(q + 1) * P], identb)
                last.then_inc(rT_p, 1)

            def tile_expert(s):
                return pe.value_load(expert[0:1, bass.ds(s, 1)], min_val=0, max_val=E - 1)

            def up(s, j):
                e = tile_expert(s)
                wait(pe, rT_s, s + 1)
                wait(pe, hid_s, TT + s - 1)
                for q in range(PARTS * C):
                    last = pe.matmul(bank[j % 2][:, 0:2 * I], rT[:, j % 2, q, :], w13[:, q % C, bass.ds(e, 1), :],
                                     start=q == 0, stop=q == PARTS * C - 1)
                last.then_inc(up_p, 1)

            def down(s, j):
                e = tile_expert(s)
                wait(pe, lo_s, TT + s + 1)
                if isinstance(s, int) and s < 2:
                    pe.wait_ge(y_s, TT + s - 1)
                else:
                    wait(pe, yo_s, s - 1)
                for k in range(2):
                    for q in range(PARTS):
                        last = pe.matmul(YP(j), hT3[0:IH, j % 2, q, k, :], w2[:, k, bass.ds(e, 1), :],
                                         start=k == 0 and q == 0, stop=k == 1 and q == PARTS - 1)
                last.then_inc(y_p, 1)

            def step(s, j, i):
                turn_hidden(TT + s, 2, IH, j)
                if not (isinstance(s, int) and s + 1 == NS):
                    up(s + 1, j + 1)
                if not (isinstance(s, int) and s + 2 >= NS):
                    turn_rows(*later(i, j, 2))
                if not (isinstance(s, int) and s == 0):
                    down(s - 1, j + 1)

            pe.wait_ge(ld_ew, 32)
            turn_rows(0, 0, 0)
            up(0, 0)
            turn_rows(1, 1, 0)
            over_tiles(pe, step, NS, RING)
            down(NS - 1, NS - 1)


_OUT = (B, N, D)


def kernel(**inputs):
    import numpy as np
    import ml_dtypes
    import concourse.bacc as bacc
    from concourse.bass_utils import run_bass_kernel_spmd as run

    a = {k: np.asarray(v) for k, v in inputs.items()}

    row = np.arange(P)
    t, h = row // GH, row % GH
    j = np.arange(KB)
    d = j[None, :] - WIN - t[:, None]
    inside = (d >= -WIN) & (d < WIN)
    m = np.where(inside, (WIN - np.abs(d) / 2.0) / WIN * HD ** -0.5, 1.0)
    cf = np.zeros((P, FCW), np.float32)
    cf[:, slice(*FC["ident"])] = np.eye(P)
    cf[:, slice(*FC["window"])] = np.tile(m.T, (BPT, 1))
    cf[:, slice(*FC["headsel"])] = ((row % GC) // HD)[:, None] == np.arange(GH)[None, :]
    cf[:, slice(*FC["nhalf"])] = -0.5
    cf[:, slice(*FC["rev"])] = E - np.arange(E)
    cf[:, slice(*FC["lane"])] = row
    cf[:, slice(*FC["tile"])] = np.arange(NS)
    cf[:, slice(*FC["turn"])] = np.arange(TOPK * TT)
    cf[:, slice(*FC["row1"])] = row[:, None] + 1
    cf[:, slice(*FC["one"])] = 1.0
    cb = np.zeros((P, BCW), np.float32)
    cb[:, 0:P] = np.eye(P)
    cb[:, BCW - 2 * P:BCW - P] = row[:, None] < row[None, :]
    cb[:, BCW - P:] = 1.0
    for u in range(U):
        key = u * P + QB * np.arange(BL)[:, None] + j[None, :] - WIN
        ok = inside.T[None, :, :] & ((key >= 0) & (key < N))[:, :, None]
        ok = ok.reshape(2, P, P).transpose(1, 0, 2)
        ok = np.broadcast_to(ok[:, None], (P, C, 2, P))
        cb[:, P + u * 4 * P:P + (u + 1) * 4 * P] = np.where(ok, 0.0, -1e30).reshape(P, -1)
    cb = cb.astype(ml_dtypes.bfloat16)

    w13 = np.concatenate([a["L0_ffn_w1"], a["L0_ffn_w3"]], axis=1)
    sw13 = np.concatenate([a["L0_ffn_sw1"], a["L0_ffn_sw3"]], axis=0)
    sw2 = np.zeros((SK * P, D), a["L0_ffn_sw2"].dtype)
    sw2[:SI] = a["L0_ffn_sw2"].T
    arrays = {
        "gateT": a["L0_ffn_gate_w"].T,
        "w13T": w13.reshape(E, 2 * I, C, P).transpose(3, 2, 0, 1),
        "w2T": a["L0_ffn_w2"].reshape(E, D, 2, IH).transpose(3, 2, 0, 1),
        "sw13T": sw13.reshape(2 * SI, C, P).transpose(2, 1, 0),
        "sw2T": sw2.reshape(SK, P, D).transpose(1, 0, 2),
        "x": a["L0_attn_x"].reshape(T, D),
        "wqkvT": a["L0_attn_qkv_w"].T,
        "projT": a["L0_attn_proj_w"].T,
        "proj_b": a["L0_attn_proj_b"].reshape(1, D),
        "cT": a["L0_c"].T,
        "wmod": a["L0_wmod"],
        "cf": cf,
        "cb": cb,
    }
    arrays = {k: np.ascontiguousarray(v) for k, v in arrays.items()}
    nc = bacc.Bacc("TRN2", target_bir_lowering=False, num_devices=1)
    args = {k: nc.dram_tensor(k, v.shape, mybir.dt.from_np(v.dtype), kind="ExternalInput").ap()
            for k, v in arrays.items()}
    out = nc.dram_tensor("out", (T, D), F32, kind="ExternalOutput").ap()
    build(nc, **args, out=out)
    r = run(nc, [arrays], core_ids=[0])
    return r.results[0]["out"].reshape(_OUT)
```

```python
from contextlib import ExitStack

import concourse.bass as bass
import numpy as np
from concourse import mybir

F32 = mybir.dt.float32
I32 = mybir.dt.int32
BF16 = mybir.dt.bfloat16
ALU = mybir.AluOpType
ACT = mybir.ActivationFunctionType
AX = mybir.AxisListType

B, N, D = 8, 256, 256
T = B * N
P = 128
C = D // P
TT = T // P
U = N // P
HEADS, HD, WIN = 32, 8, 8

QB = 16
KB = 2 * QB
GH = P // QB
GC = GH * HD
G = D // GC
BL = P // QB
NBLK = G * BL
BPT = P // KB
NQ = BPT
PADN = WIN + N + WIN
EPS = 1e-5

E, I, SI, TOPK = 16, 176, 352, 2
IH = I // 2
SK = -(-SI // P)
PARTS = 3
NS = T * TOPK // P + E
RING = 4
AHEAD = RING
SHARED_W = (P, SK)
EXPERT_W = (IH, 2)
AT_RANK, AT_SLOT = 4, 11
NONE = 2 * TOPK * T

FC = {}
_w = 0
for _n, _k in (("ident", P), ("window", P), ("headsel", GH), ("nhalf", 2), ("rev", E), ("lane", P), ("tile", NS),
               ("turn", TOPK * TT), ("row1", 1), ("one", E)):
    FC[_n] = (_w, _w + _k)
    _w += _k
FCW = _w
BCW = P + 2 * 4 * P + 2 * P


def build(nc, x, wqkvT, projT, proj_b, cT, wmod, gateT, w13T, w2T, sw13T, sw2T, cf, cb, out):
    ctx = ExitStack()
    with ctx:
        def sb(name, shape, dt=F32):
            return ctx.enter_context(nc.sbuf_tensor(name, shape, dt))

        def sem(name):
            return ctx.enter_context(nc.semaphore(name))

        class Region:

            def __init__(self, tensor):
                self.tensor, self.at = tensor, 0

            def take(self, pattern, shape, dt=F32):
                n = int(np.prod([v for v in shape])) * (2 if dt == BF16 else 4) // 4
                v = self.tensor[:, self.at:self.at + n]
                self.at += n
                assert self.at <= self.tensor.shape[1]
                if dt != F32:
                    v = v.bitcast(dt)
                if len(shape) == 1:
                    return v
                names = pattern.split()
                return v.rearrange(f"p ({pattern}) -> p {pattern}", **dict(zip(names[1:], shape[1:])))

        first_region = sb("first_region", [P, C * 6 * D])
        setup = Region(first_region)
        picks = Region(first_region)
        second_region = sb("second_region", [P, 6720])
        attn = Region(second_region)
        late = Region(second_region)
        xs = sb("xs", [P, TT, D])
        cft = sb("cft", [P, FCW])
        cbt = sb("cbt", [P, BCW], BF16)
        wqkv = attn.take("c n", (C, 3 * D,))
        wpj = attn.take("c n", (C, D,))
        pb = sb("pb", [1, D])
        ones_row = sb("ones_row", [1, P])
        cts = sb("cts", [P, C, B])
        csig = sb("csig", [P, C, B])
        wms = setup.take("c n", (C, 6 * D,))
        modrow = sb("modrow", [B, 6 * D])
        gtmp = sb("gtmp", [B, 4, D])
        modT = sb("modT", [P, 4, B])
        modb = sb("modb", [P, B, 4 * D])

        bst2 = sb("bst2", [P, U, 6])
        mv2 = sb("mv2", [P, U, 2])
        ve2 = sb("ve2", [P, U])
        rstd2s = sb("rstd2s", [P, U])
        bst = sb("bst", [P, U, 6])
        mv = sb("mv", [P, U, 2])
        ve = sb("ve", [P, U])
        rstd = sb("rstd", [P, U])
        xn = attn.take("u d", (U, D,))
        hT = attn.take("c n", (C, PADN,))
        hw = attn.take("c b j", (C, N // QB, KB,))
        region = sb("region", [P, C * N * GH + 4 * 2048])
        at = C * N * GH
        qbd = region[:, 0:at].rearrange("p (c n h) -> p c n h", c=C, h=GH)
        kT = attn.take("c n", (C, PADN,))
        vw = attn.take("w d", (N // (QB * BPT), D,))
        ST = region[:, at:at + 2048].rearrange("p (u k j) -> p u k j", u=U, j=P)
        S = region[:, at + 2048:at + 4096].rearrange("p (u k j) -> p u k j", u=U, j=KB)
        mx = sb("mx", [P, U, NBLK])
        rs = sb("rs", [P, U, NBLK])
        ri = sb("ri", [P, U, NBLK])
        PT = region[:, at + 4096:at + 6144].rearrange("p (u k j) -> p u k j", u=U, j=P)
        Z = region[:, at + 6144:at + 8192].rearrange("p (z k h) -> p z k h", z=NQ, h=GH)
        w13n, w2n = C * E * SI // 2, 2 * E * D // 2
        w13 = region[:, 0:w13n].bitcast(BF16).rearrange("p (c e i) -> p c e i", c=C, e=E)
        w2 = region[0:IH, w13n:w13n + w2n].bitcast(BF16).rearrange("p (k e d) -> p k e d", k=2, e=E)
        yk = region[:, 0:TOPK * TT * D].rearrange("p (k t d) -> p k t d", k=TOPK, t=TT)
        OT = attn.take("u c t", (U, C, P,))
        ao = attn.take("u d", (U, D,))

        h2 = sb("h2", [P, U, D])
        hr = sb("hr", [P, U, D])
        h3 = sb("h3", [P, U, PARTS, D], BF16)
        xT = sb("xT", [P, TT, PARTS * C, P], BF16)
        gws = sb("gws", [P, C, E])
        gwr = sb("gwr", [P, C, E])
        gw3 = sb("gw3", [P, C, PARTS, E], BF16)
        sw13 = sb("sw13", [P, C, 2 * SI], BF16)
        sw2 = sb("sw2", [P, SK, D], BF16)
        logit = sb("logit", [P, TT, E])
        score = sb("score", [P, TT, E])
        cand = sb("cand", [P, TT, E])
        oh = sb("oh", [P, TOPK, TT, E])
        ohb = sb("ohb", [P, TT + 1, E], BF16)
        top = sb("top", [P, TOPK, TT])
        rtop = sb("rtop", [P, TOPK, TT])
        gatew = sb("gatew", [P, TOPK, TT])
        den = sb("den", [P, TT])
        cnt = sb("cnt", [P, 4, E])
        cnti = sb("cnti", [P, E], I32)
        pos = sb("pos", [P, TOPK * TT])
        posi = sb("posi", [P, 3, TOPK * TT], I32)
        posf = sb("posf", [P, 2, TOPK * TT])
        lane_oh = picks.take("k l", (TOPK * TT, P,), BF16)
        tile_oh = picks.take("k s", (TOPK * TT, NS,), BF16)
        val = late.take("k v s", (TOPK * TT, 2, NS,), BF16)
        owner = late.take("s e", (NS, E,))
        slot = sb("slot", [P, 4, NS])
        sloti = sb("sloti", [P, 2, NS], I32)
        expert = sb("expert", [P, NS + 2], I32)
        ixg = sb("ixg", [P, RING], I32)
        ixp = sb("ixp", [P, RING], I32)
        rows = late.take("j n", (RING, PARTS * D,), BF16)
        rT = late.take("j q t", (2, PARTS * C, P,), BF16)
        act_s = late.take("j w", (2, SI,))
        hid = sb("hid", [P, 2, SK * P])
        hres = late.take("j k t", (2, SK, P,))
        hT3 = sb("hT3", [P, 2, PARTS, SK, P], BF16)
        yo = sb("yo", [P, RING, D])

        ident = cft[:, FC["ident"][0]:FC["ident"][1]]
        window = cft[:, FC["window"][0]:FC["window"][1]]
        headsel = cft[:, FC["headsel"][0]:FC["headsel"][1]]
        nhalf = cft[:, FC["nhalf"][0]:FC["nhalf"][1]]
        rev, lane, tileno, turn, row1, one = (cft[:, FC[n][0]:FC[n][1]] for n in (
            "rev", "lane", "tile", "turn", "row1", "one"))
        identb = cbt[:, 0:P]
        before = cbt[:, BCW - 2 * P:BCW - P]
        onesb = cbt[:, BCW - P:BCW]

        def addmask(u):
            return cbt[:, P + u * 4 * P:P + (u + 1) * 4 * P]

        bank = [ctx.enter_context(nc.psum_tensor(f"bank{i}", [P, 1024], F32)) for i in range(4)]
        SP = [bank[0], bank[1]]
        ZP = bank[2]
        M0 = bank[3][:, 0:512]
        M1 = bank[3][:, 512:1024]

        MB = [ZP[:, u * 512:u * 512 + PARTS * D // 2].bitcast(BF16) for u in range(U)]
        LG = [ZP[:, u * 512 + PARTS * D // 2:u * 512 + PARTS * D // 2 + PARTS * E] for u in range(U)]

        def HT(j):
            return bank[2][:, (j % 2) * 512:(j % 2) * 512 + SK * P].rearrange("p (k t) -> p k t", t=P)

        def YP(j):
            return bank[3][:, (j % 2) * 512:(j % 2) * 512 + D]

        def spare(t):
            return bank[3][:, (t % 2) * 512:(t % 2 + 1) * 512]

        def RTP(j):
            return bank[j % 2][:, 512:512 + PARTS * D // 2].bitcast(BF16)

        moddram = nc.dram_tensor("moddram", [B, 6 * D], F32, kind="Internal").ap()

        hrows = nc.dram_tensor("hrows", [T, PARTS * D], BF16, kind="Internal").ap()
        yrows = nc.dram_tensor("yrows", [TOPK * T, D], F32, kind="Internal").ap()

        l2_st, l2_mv, l2_ve, l2_rs, l2_xn, l2_mu, l2_h = (sem("l2_" + n) for n in (
            "st", "mv", "ve", "rs", "xn", "mu", "h"))
        p_hi, p_r, p_mid, p_lo, xT_p, xT_s, lg_p, lg_s, st_h = (sem(n) for n in (
            "p_hi", "p_r", "p_mid", "p_lo", "xT_p", "xT_s", "lg_p", "lg_s", "st_h"))
        ld_g, ld_sw, ld_ew, gw_s = (sem(n) for n in ("ld_g", "ld_sw", "ld_ew", "gw_s"))
        r_exp, rt, rank_p, slot_p, routed, ohb_s = (sem(n) for n in (
            "r_exp", "rt", "rank_p", "slot_p", "routed", "ohb_s"))
        rank_s, who_s = sem("rank_s"), sem("who_s")
        val_s, passed = sem("val_s"), sem("passed")
        up_p, silu_s, hid_s, ht_p, hi_s, res_s, mid_s, lo_s, y_p, y_s = (sem("m_" + n) for n in (
            "up", "silu", "hid", "ht", "hi", "res", "mid", "lo", "y", "ys"))
        sh_s = sem("sh_s")
        ixg_s, ixp_s, rT_p, rT_s, yo_s = (sem(n) for n in ("ixg_s", "ixp_s", "rT_p", "rT_s", "yo_s"))
        fetch = [sem(f"fetch{k}") for k in range(RING)]
        put = [sem(f"put{k}") for k in range(RING)]
        ld_y = [sem(f"ld_y{k}") for k in range(B)]
        f_a, f_b, f_c, f_d = (sem("f_" + n) for n in "abcd")

        ld_c, ld_x0, ld_x1, ld_w = (sem("ld_" + n) for n in ("c", "x0", "x1", "w"))
        ld_wm = [sem(f"ld_wm{k}") for k in range(3)]
        mod_c = sem("mod_c")
        c_exp, c_den, c_inv, c_silu = (sem("c_" + n) for n in ("exp", "den", "inv", "silu"))
        mod_p, mod_r, g_sgn, g_abs, g_fin, modT_p, modT_s, mod_st, mod_ld = (sem(n) for n in (
            "mod_p", "mod_r", "g_sgn", "g_abs", "g_fin", "modT_p", "modT_s", "mod_st", "mod_ld"))
        pads, hw_s = sem("pads"), sem("hw_s")
        ln_st, ln_mv, ln_ve, ln_rs, ln_xn = (sem("ln_" + n) for n in ("st", "mv", "ve", "rs", "xn"))
        hT_p, hT_s, q_p, q_s, k_p, k_s, v_p, v_s = (sem(n) for n in (
            "hT_p", "hT_s", "q_p", "q_s", "k_p", "k_s", "v_p", "v_s"))
        s_p, s_m, st_p, s_mx, s_sub, s_ex, s_sum, s_ri = (sem("s_" + n) for n in (
            "p", "m", "t", "mx", "sub", "ex", "sum", "ri"))
        s_nm = [sem(f"s_nm{u}") for u in range(U)]
        pt_p, pt_s, z_p, z_s, o_s, pr_p, ga_s, x1_s = (sem(n) for n in (
            "pt_p", "pt_s", "z_p", "z_s", "o_s", "pr_p", "ga_s", "x1_s"))
        st_out = sem("st_out")

        block = ctx.enter_context(nc.Block())

        def wait(eng, s, v):
            if not (isinstance(v, int) and v <= 0):
                eng.wait_ge(s, v)

        def settle(eng):
            eng.sem_inc(passed, 1)

        def over(eng, main):
            main(0, True, 2)
            with eng.Fori(1, B - 2) as it:
                main(it, False, 2)
            main(B - 2, False, 1)
            main(B - 1, False, 0)

        def over_tiles(eng, step, n, k):
            for j in range(k):
                step(j, j, 0)
            with eng.Fori(1, n // k - 1) as i:
                for j in range(k):
                    step(k * i + j, j, i)
            for j in range(k):
                step(n - k + j, j, n // k - 1)

        def later(i, j, d):
            q, r = divmod(j + d, RING)
            return RING * (i + q) + r, r, i + q

        x_t = x.rearrange("(t p) d -> p t d", p=P)

        @block.sync
        def _(sp):
            sp.dma_start(cts[:, :, :], cT.rearrange("(c p) b -> p c b", p=P)).then_inc(ld_c, 16)
            wmod_t = wmod.rearrange("(c p) n -> p c n", p=P)
            for k in range(3):
                sp.dma_start(wms[:, :, k * 512:(k + 1) * 512], wmod_t[:, :, k * 512:(k + 1) * 512]).then_inc(ld_wm[k], 16)
            sp.dma_start(xs[:, 0:U, :], x_t[:, 0:U, :]).then_inc(ld_x0, 16)
            sp.dma_start(xs[:, U:TT, :], x_t[:, U:TT, :]).then_inc(ld_x1, 16)
            sp.wait_ge(g_fin, 1)
            sp.dma_start(moddram, modrow[:, :]).then_inc(mod_st, 16)
            sp.wait_ge(mod_st, 16)
            sp.dma_start(modb[:, :, :], moddram[:, 2 * D:6 * D].partition_broadcast(P)).then_inc(mod_ld, 16)
            hrows_t = hrows.rearrange("(b u p) k -> b p u k", u=U, p=P)
            def store_h(b):
                wait(sp, p_lo, b + 1)
                sp.dma_start(hrows_t[b], h3[:, :, :, :].rearrange("p u k d -> p u (k d)")).then_inc(st_h, 16)
            store_h(0)
            with sp.Fori(1, B) as b:
                store_h(b)
            sp.wait_ge(x1_s, TT)
            sp.dma_start(w13, w13T).then_inc(ld_ew, 16)
            sp.dma_start(w2, w2T).then_inc(ld_ew, 16)
            y_t = yrows.rearrange("(k b u p) d -> b p k u d", k=TOPK, u=U, p=P)
            sp.wait_ge(y_p, TT + NS)
            for k in range(RING):
                sp.wait_ge(put[k], 16 * (NS // RING))
            for b in range(B):
                for k in range(TOPK):
                    sp.dma_start(yk[:, k, U * b:U * b + U, :], y_t[b, :, k]).then_inc(ld_y[b], 16)
            out_t = out.rearrange("(b u p) d -> b p u d", u=U, p=P)
            for b in range(B):
                sp.wait_ge(f_d, b + 1)
                sp.dma_start(out_t[b], xs[:, U * b:U * b + U, :]).then_inc(st_out, 16)
            sp.wait_ge(st_out, 16 * B)

        @block.gpsimd
        def _(gp):
            gp.memset(ones_row[:, :], 1.0)
            gp.memset(ohb[:, TT, :], 0.0)
            gp.memset(expert[:, :], 0)
            gp.memset(hid[:, :, :], 0.0)
            gp.memset(hT[:, :, :], 0.0)
            gp.memset(kT[:, :, :], 0.0).then_inc(pads, 1)
            gp.wait_ge(ld_w, 80)

            def rstd1(b):
                wait(gp, ln_ve, b + 1)
                gp.tensor_tensor(rstd[:, :], ve[:, :], nhalf, ALU.pow).then_inc(ln_rs, 1)

            def rstd2(b):
                wait(gp, l2_ve, b + 1)
                gp.tensor_tensor(rstd2s[:, :], ve2[:, :], nhalf, ALU.pow).then_inc(l2_rs, 1)

            def split(b):
                wait(gp, l2_xn, b + 1)
                gp.tensor_tensor(h2[:, :, :], h2[:, :, :],
                                 modb[:, b, 2 * D:3 * D].unsqueeze(1).to_broadcast([P, U, D]), ALU.mult).then_inc(l2_mu, 1)
                wait(gp, l2_mu, b + 1)
                gp.tensor_tensor(h2[:, :, :], h2[:, :, :],
                                 modb[:, b, D:2 * D].unsqueeze(1).to_broadcast([P, U, D]), ALU.add).then_inc(l2_h, 1)
                wait(gp, p_hi, b + 1)
                gp.tensor_tensor(hr[:, :, :], h2[:, :, :], h3[:, :, 0], ALU.subtract).then_inc(p_r, 1)

            def last_part(b):
                wait(gp, p_mid, b + 1)
                gp.tensor_tensor(h3[:, :, 2], hr[:, :, :], h3[:, :, 1], ALU.subtract).then_inc(p_lo, 1)

            def main(it, first, after):
                if first:
                    gp.wait_ge(mod_ld, 16)
                else:
                    split(it - 1)
                wait(gp, s_ri, U * it + 1)
                gp.tensor_tensor(S[:, 0], S[:, 0], ri[:, 0, :].unsqueeze(2).to_broadcast([P, NBLK, KB]),
                                 ALU.mult).then_inc(s_nm[0], 1)
                if not first:
                    last_part(it - 1)
                if after > 1:
                    rstd1(it + 2)
                rstd2(it)

            rstd1(0)
            gp.wait_ge(hT_s, 1)
            for c in range(C):
                a = hT[:, c, :]
                last = gp.tensor_copy(hw[:, c], bass.AP(a.tensor, a.offset, [a.ap[0], [QB, N // QB], [1, KB]]))
            last.then_inc(hw_s, 1)
            rstd1(1)
            over(gp, main)
            split(B - 1)
            last_part(B - 1)

            gp.wait_ge(st_h, 16 * B)
            gp.wait_ge(routed, 1)

            def get(s, j, i):
                wait(gp, rT_p, s - RING + 1)
                settle(gp)
                wait(gp, ixg_s, s + 1)
                settle(gp)
                gp.indirect_dma_start(rows[:, j, :], None, hrows,
                                      bass.IndirectOffsetOnAxis(ap=ixg[:, j:j + 1], axis=0)).then_inc(fetch[j], 16)

            def give(s, j, i):
                wait(gp, yo_s, s + 1)
                settle(gp)
                wait(gp, ixp_s, s + 1)
                settle(gp)
                gp.indirect_dma_start(yrows, bass.IndirectOffsetOnAxis(ap=ixp[:, j:j + 1], axis=0),
                                      yo[:, j, :], None, bounds_check=TOPK * T - 1,
                                      oob_is_err=False).then_inc(put[j], 16)

            def step(s, j, i):
                if not (isinstance(s, int) and s + AHEAD >= NS):
                    get(*later(i, j, AHEAD))
                if not (isinstance(s, int) and s < 2):
                    give(*later(i, j, -2))

            for s in range(AHEAD):
                get(s, s, 0)
            over_tiles(gp, step, NS, RING)
            for s in (NS - 2, NS - 1):
                give(s, s % RING, s // RING)

            for b in range(B):
                gp.wait_ge(f_b, b + 1)
                v = yk[:, 0, U * b:U * b + U, :]
                gp.tensor_tensor(v, v, modb[:, b, 3 * D:].unsqueeze(1).to_broadcast([P, U, D]),
                                 ALU.mult).then_inc(f_c, 1)

        @block.scalar
        def _(act):
            act.dma_start(cft[:, :], cf).then_inc(ld_w, 16)
            act.dma_start(wqkv[:, :, :], wqkvT.rearrange("(c p) n -> p c n", p=P)).then_inc(ld_w, 16)
            act.wait_ge(ld_c, 16)
            act.activation(csig[:, :, :], cts[:, :, :], ACT.Exp, scale=-1.0).then_inc(c_exp, 1)
            act.dma_start(cbt[:, :], cb).then_inc(ld_w, 16)
            act.dma_start(wpj[:, :, :], projT.rearrange("(c p) n -> p c n", p=P)).then_inc(ld_w, 16)
            act.dma_start(pb[:, :], proj_b).then_inc(ld_w, 16)
            act.dma_start(gws[:, :, :], gateT.rearrange("(c p) e -> p c e", p=P)).then_inc(ld_g, 16)
            act.dma_start(sw13[:, :, :], sw13T).then_inc(ld_sw, 16)
            act.dma_start(sw2[:, :, :], sw2T).then_inc(ld_sw, 16)

            def scaled_h(b):
                wait(act, hT_p, b + 1)
                if isinstance(b, int) and b == 0:
                    act.wait_ge(pads, 1)
                    act.wait_ge(modT_s, 1)
                wait(act, k_p, b)
                wait(act, hw_s, b)
                for c in range(C):
                    last = act.activation(hT[:, c, WIN:WIN + N], M0[:, c * N:(c + 1) * N], ACT.Identity,
                                          scale=modT[:, 2 + c, bass.ds(b, 1)], bias=modT[:, c, bass.ds(b, 1)])
                last.then_inc(hT_s, 1)

            def spread_q(b, c):
                if c == 0:
                    wait(act, q_p, b + 1)
                    wait(act, s_p, U * b)
                for h in range(GH):
                    last = act.activation(qbd[:, c, :, h], M1[:, c * N:(c + 1) * N], ACT.Copy,
                                          scale=headsel[:, h:h + 1])
                if c == C - 1:
                    last.then_inc(q_s, 1)

            def keep_k(b):
                wait(act, k_p, b + 1)
                for c in range(C):
                    last = act.activation(kT[:, c, WIN:WIN + N], M0[:, c * N:(c + 1) * N], ACT.Copy)
                last.then_inc(k_s, 1)

            def key_windows(b):
                wait(act, hT_s, b + 1)
                wait(act, v_p, U * b)
                settle(act)
                for c in range(C):
                    a = hT[:, c, :]
                    last = act.activation(hw[:, c], bass.AP(a.tensor, a.offset, [a.ap[0], [QB, N // QB], [1, KB]]), ACT.Copy)
                last.then_inc(hw_s, 1)

            def keep_v(b, u):
                wait(act, v_p, U * b + u + 1)
                wait(act, z_p, NQ * U * b)
                act.activation(vw[:, 2 * u:2 * u + 2, :], ZP[:, 2 * u * D:2 * (u + 1) * D], ACT.Copy).then_inc(v_s, 1)

            def turned_p(it, u):
                n = U * it + u
                wait(act, pt_p, n + 1)
                wait(act, z_p, NQ * (n - U + 1))
                act.activation(PT[:, u], SP[u][:, :], ACT.Copy).then_inc(pt_s, 1)

            def first_part(b):
                wait(act, l2_h, b + 1)
                act.activation(h3[:, :, 0], h2[:, :, :], ACT.Copy).then_inc(p_hi, 1)

            def second_part(b):
                wait(act, p_r, b + 1)
                act.activation(h3[:, :, 1], hr[:, :, :], ACT.Copy).then_inc(p_mid, 1)

            def turned_parts(b):
                wait(act, xT_p, b + 1)
                for u in range(U):
                    last = act.activation(xT[:, U * b + u].rearrange("p q t -> p (q t)"), MB[u], ACT.Copy)
                last.then_inc(xT_s, 1)

            def exponent(it, u):
                wait(act, s_sub, U * it + u + 1)
                act.activation(S[:, u], S[:, u], ACT.Exp).then_inc(s_ex, 1)

            def main(it, first, after):
                if after:
                    scaled_h(it + 1)
                exponent(it, 0)
                if not first:
                    first_part(it - 1)
                    second_part(it - 1)
                keep_v(it, 0)
                exponent(it, 1)
                turned_p(it, 0)
                keep_v(it, 1)
                if after:
                    spread_q(it + 1, 0)
                turned_p(it, 1)
                if after:
                    spread_q(it + 1, 1)
                    keep_k(it + 1)
                    key_windows(it + 1)
                if not first:
                    turned_parts(it - 1)
                    wait(act, st_h, 16 * it)

            scaled_h(0)
            spread_q(0, 0)
            spread_q(0, 1)
            over(act, main)
            first_part(B - 1)
            second_part(B - 1)
            turned_parts(B - 1)

            act.wait_ge(lg_s, B)
            act.activation(score[:, :, :], logit[:, :, :], ACT.Exp, scale=-1.0).then_inc(r_exp, 1)

            def silu(n, w, j):
                wait(act, up_p, n + 1)
                wait(act, hid_s, n - 1)
                act.activation(act_s[:, j % 2, 0:w], bank[j % 2][:, 0:w], ACT.Silu).then_inc(silu_s, 1)

            def hi(n, w, j):
                p, k = w
                wait(act, ht_p, n + 1)
                wait(act, y_p, n - 1)
                act.activation(hT3[0:p, j % 2, 0, 0:k], HT(j)[0:p, 0:k], ACT.Copy).then_inc(hi_s, 1)

            def mid(n, w, j):
                p, k = w
                wait(act, res_s, n + 1)
                act.activation(hT3[0:p, j % 2, 1, 0:k], hres[0:p, j % 2, 0:k], ACT.Copy).then_inc(mid_s, 1)

            def shared(t, j, i):
                hi(t, SHARED_W, j)
                if not (isinstance(t, int) and t in (0, TT - 1)):
                    silu(t + 1, SI, j + 1)
                mid(t, SHARED_W, j)

            silu(0, SI, 0)
            silu(1, SI, 1)
            over_tiles(act, shared, TT, 2)

            def result(s, j, i):
                wait(act, y_p, TT + s + 1)
                wait(act, put[j], 16 * i)
                if isinstance(s, int) and s == 0:
                    act.wait_ge(sh_s, TT)
                act.activation(yo[:, j, :], YP(j), ACT.Copy).then_inc(yo_s, 1)

            def step(s, j, i):
                hi(TT + s, EXPERT_W, j)
                if not (isinstance(s, int) and s + 1 == NS):
                    silu(TT + s + 1, I, j + 1)
                mid(TT + s, EXPERT_W, j)
                if not (isinstance(s, int) and s == 0):
                    result(*later(i, j, -1))

            silu(TT, I, 0)
            over_tiles(act, step, NS, RING)
            result(NS - 1, RING - 1, NS // RING - 1)

            for b in range(B):
                act.wait_ge(ld_y[b], 16 * TOPK)
                for u in range(U):
                    last = act.activation(yk[:, 0, U * b + u], yk[:, 0, U * b + u], ACT.Copy,
                                          scale=gatew[:, 0, U * b + u:U * b + u + 1])
                last.then_inc(f_a, 1)

        @block.vector
        def _(dve):
            def stats(xt, k):
                for u in range(U):
                    last = dve.bn_stats(bst[:, u], xt(u))
                last.then_inc(ln_st, 1)
                wait(dve, ln_st, k)
                settle(dve)
                for u in range(U):
                    last = dve.bn_aggr(mv[:, u], bst[:, u])
                last.then_inc(ln_mv, 1)
                wait(dve, ln_mv, k)
                dve.tensor_scalar(ve[:, :], mv[:, :, 1], EPS, None, ALU.add).then_inc(ln_ve, 1)

            def ln1_stats(b):
                stats(lambda u: xs[:, U * b + u, :], b + 1)

            def ln1_apply(b):
                wait(dve, ln_rs, b + 1)
                wait(dve, hT_p, b)
                for u in range(U):
                    last = dve.tensor_scalar(xn[:, u], xs[:, U * b + u, :], mv[:, u, 0:1], rstd[:, u:u + 1],
                                             ALU.subtract, ALU.mult)
                last.then_inc(ln_xn, 1)

            dve.wait_ge(c_exp, 1)
            dve.tensor_scalar(csig[:, :, :], csig[:, :, :], 1.0, None, ALU.add).then_inc(c_den, 1)
            dve.wait_ge(c_den, 1)
            dve.reciprocal(csig[:, :, :], csig[:, :, :]).then_inc(c_inv, 1)
            dve.wait_ge(c_inv, 1)
            dve.tensor_tensor(cts[:, :, :], cts[:, :, :], csig[:, :, :], ALU.mult).then_inc(c_silu, 1)
            dve.wait_ge(mod_p, 1)
            dve.tensor_copy(modrow[:, 0:D], bank[0][0:B, 0:D])
            dve.tensor_scalar(modrow[:, D:2 * D], bank[0][0:B, D:2 * D], 1.0, None, ALU.add).then_inc(mod_c, 1)
            dve.wait_ge(ld_x0, 16)
            ln1_stats(0)
            ln1_apply(0)
            dve.wait_ge(mod_p, 3)
            dve.tensor_copy(modrow[:, 2 * D:4 * D], bank[0][0:B, 512:1024])
            dve.tensor_scalar(modrow[:, 4 * D:5 * D], bank[1][0:B, 0:D], 1.0, None, ALU.add)
            dve.tensor_copy(modrow[:, 5 * D:6 * D], bank[1][0:B, D:2 * D]).then_inc(mod_r, 1)
            dve.wait_ge(modT_p, 1)
            dve.tensor_copy(modT[:, :, :], M1[:, 0:4 * B]).then_inc(modT_s, 1)
            dve.wait_ge(mod_r, 1)
            for i, k in enumerate((2, 5)):
                g = modrow[:, k * D:(k + 1) * D]
                dve.tensor_scalar(gtmp[:, i], g, 0.0, 2.0, ALU.is_ge, ALU.mult)
                last = dve.scalar_tensor_tensor(gtmp[:, 2 + i], g, -1.0, g, ALU.mult, ALU.max)
            last.then_inc(g_sgn, 1)
            dve.wait_ge(g_sgn, 1)
            dve.tensor_scalar(gtmp[:, 0:2], gtmp[:, 0:2], -1.0, None, ALU.add)
            dve.tensor_scalar(gtmp[:, 2:4], gtmp[:, 2:4], 0.25, None, ALU.max).then_inc(g_abs, 1)
            dve.wait_ge(g_abs, 1)
            for i, k in enumerate((2, 5)):
                last = dve.tensor_tensor(modrow[:, k * D:(k + 1) * D], gtmp[:, i], gtmp[:, 2 + i], ALU.mult)
            last.then_inc(g_fin, 1)
            def logits(b):
                wait(dve, lg_p, b + 1)
                for u in range(U):
                    last = dve.tensor_reduce(logit[:, U * b + u, :], LG[u].rearrange("p (k e) -> p e k", e=E),
                                             AX.X, ALU.add)
                last.then_inc(lg_s, 1)

            def own_heads(it, k):
                if k < NQ * U:
                    u, r = divmod(k, NQ)
                    n = U * it + u
                    wait(dve, z_p, NQ * U * it + k + 1)
                    dve.tensor_tensor(Z[:, r], ZP[:, (r % 2) * 512:(r % 2 + 1) * 512].rearrange("p (k h) -> p k h", h=GH),
                                      headsel.unsqueeze(1).to_broadcast([P, 512 // GH, GH]), ALU.mult).then_inc(z_s, 1)
                if k > 0:
                    u, r = divmod(k - 1, NQ)
                    n = U * it + u
                    wait(dve, z_s, NQ * U * it + k)
                    if r == 0:
                        wait(dve, pr_p, n - U + 1)
                    ov = OT[:, u].rearrange("p c (q r t) -> p r q c t", q=2, r=BPT)
                    last = dve.tensor_reduce(ov[:, r], Z[:, r].rearrange("p (q c t) h -> p q c t h", q=2, c=C),
                                             AX.X, ALU.add)
                    if r == NQ - 1:
                        last.then_inc(o_s, 1)

            def by_window(it, u):
                n = U * it + u
                wait(dve, s_p, n + 1)
                wait(dve, st_p, n - U + 1)
                dve.tensor_tensor(ST[:, u], SP[u][:, :].rearrange("p (k j) -> p k j", j=P),
                                  window.unsqueeze(1).to_broadcast([P, NBLK // BPT, P]), ALU.mult).then_inc(s_m, 1)

            def less_maximum(it, u):
                n = U * it + u
                wait(dve, st_p, n + 1)
                sv = SP[u][:, :].rearrange("p (k j) -> p k j", j=KB)
                dve.tensor_reduce(mx[:, u], sv, AX.X, ALU.max).then_inc(s_mx, 1)
                wait(dve, s_mx, n + 1)
                wait(dve, pt_p, n - U + 1)
                dve.tensor_tensor(S[:, u], sv, mx[:, u, :].unsqueeze(2).to_broadcast([P, NBLK, KB]),
                                  ALU.subtract).then_inc(s_sub, 1)

            def one_over_sum(it, u):
                n = U * it + u
                wait(dve, s_ex, n + 1)
                dve.tensor_reduce(rs[:, u], S[:, u], AX.X, ALU.add).then_inc(s_sum, 1)
                wait(dve, s_sum, n + 1)
                dve.reciprocal(ri[:, u], rs[:, u]).then_inc(s_ri, 1)

            def residual(it, u):
                n = U * it + u
                wait(dve, pr_p, n + 1)
                dve.tensor_tensor(ao[:, u], SP[u][:, 512:512 + D], modb[:, it, 0:D], ALU.mult).then_inc(ga_s, 1)
                wait(dve, ga_s, n + 1)
                dve.tensor_tensor(xs[:, n, :], xs[:, n, :], ao[:, u], ALU.add).then_inc(x1_s, 1)

            def main(it, first, after):
                less_maximum(it, 0)
                by_window(it, 1)
                one_over_sum(it, 0)
                less_maximum(it, 1)
                if after > 1:
                    ln1_stats(it + 2)
                one_over_sum(it, 1)
                wait(dve, s_ri, U * it + 2)
                dve.tensor_tensor(S[:, 1], S[:, 1], ri[:, 1, :].unsqueeze(2).to_broadcast([P, NBLK, KB]),
                                  ALU.mult).then_inc(s_nm[1], 1)
                for k in range(NQ * U + 1):
                    own_heads(it, k)
                    if k == NQ * U - 2:
                        if first:
                            dve.wait_ge(mod_ld, 16)
                        residual(it, 0)
                if after > 1:
                    ln1_apply(it + 2)
                if after:
                    by_window(it + 1, 0)
                residual(it, 1)
                wait(dve, x1_s, U * it + U)
                settle(dve)
                for u in range(U):
                    last = dve.bn_stats(bst2[:, u], xs[:, U * it + u, :])
                last.then_inc(l2_st, 1)
                wait(dve, l2_st, it + 1)
                settle(dve)
                for u in range(U):
                    last = dve.bn_aggr(mv2[:, u], bst2[:, u])
                last.then_inc(l2_mv, 1)
                wait(dve, l2_mv, it + 1)
                dve.tensor_scalar(ve2[:, :], mv2[:, :, 1], EPS, None, ALU.add).then_inc(l2_ve, 1)
                wait(dve, l2_rs, it + 1)
                wait(dve, p_r, it)
                for u in range(U):
                    last = dve.tensor_scalar(h2[:, u], xs[:, U * it + u, :], mv2[:, u, 0:1], rstd2s[:, u:u + 1],
                                             ALU.subtract, ALU.mult)
                last.then_inc(l2_xn, 1)
                if not first:
                    logits(it - 1)

            dve.wait_ge(k_p, 1)
            dve.wait_ge(pads, 1)
            for c in range(C):
                last = dve.tensor_copy(kT[:, c, WIN:WIN + N], M0[:, c * N:(c + 1) * N])
            last.then_inc(k_s, 1)
            dve.wait_ge(ld_x1, 16)
            ln1_stats(1)
            ln1_apply(1)
            dve.wait_ge(ld_g, 16)
            for k in range(PARTS):
                dve.tensor_copy(gw3[:, :, k, :], gws[:, :, :]).then_inc(gw_s, 1)
                if k < PARTS - 1:
                    dve.wait_ge(gw_s, 2 * k + 1)
                    dve.tensor_tensor(gws[:, :, :], gws[:, :, :], gw3[:, :, k, :], ALU.subtract).then_inc(gw_s, 1)
                    dve.wait_ge(gw_s, 2 * k + 2)
            by_window(0, 0)
            over(dve, main)
            logits(B - 1)

            links = [0]

            def link(ins):
                links[0] += 1
                ins.then_inc(rt, 1)
                dve.wait_ge(rt, links[0])

            revb = rev.unsqueeze(1).to_broadcast([P, TT, E])
            TK = TOPK * TT

            def best(k):
                link(dve.tensor_reduce(top[:, k], score[:, :, :], AX.X, ALU.max))
                link(dve.tensor_tensor(cand[:, :, :], score[:, :, :],
                                       top[:, k].unsqueeze(2).to_broadcast([P, TT, E]), ALU.is_equal))

            def lowest():
                link(dve.tensor_tensor(cand[:, :, :], cand[:, :, :], revb, ALU.mult))

            def chosen(k):
                link(dve.tensor_reduce(rtop[:, k], cand[:, :, :], AX.X, ALU.max))
                link(dve.tensor_tensor(oh[:, k], rtop[:, k].unsqueeze(2).to_broadcast([P, TT, E]), revb,
                                       ALU.is_equal))

            def places_onehot(k):
                dve.tensor_tensor(lane_oh[:, k * TT:(k + 1) * TT, :], lane.unsqueeze(1).to_broadcast([P, TT, P]),
                                  posf[:, 0, k * TT:(k + 1) * TT].unsqueeze(2).to_broadcast([P, TT, P]), ALU.is_equal)

            def route(stage):
                if stage == 0:
                    dve.wait_ge(r_exp, 1)
                    link(dve.tensor_scalar(score[:, :, :], score[:, :, :], 1.0, None, ALU.add))
                    link(dve.reciprocal(score[:, :, :], score[:, :, :]))
                elif stage == 1:
                    best(0)
                    lowest()
                    chosen(0)
                elif stage == 2:
                    link(dve.scalar_tensor_tensor(score[:, :, :], oh[:, 0], -2.0, score[:, :, :], ALU.mult, ALU.add))
                    best(1)
                    lowest()
                elif stage == 3:
                    chosen(1)
                    dve.tensor_tensor(ohb[:, 0:TT, :], oh[:, 0], oh[:, 1], ALU.add).then_inc(ohb_s, 1)
                elif stage == 4:
                    link(dve.tensor_tensor(den[:, :], top[:, 0], top[:, 1], ALU.add))
                    link(dve.reciprocal(den[:, :], den[:, :]))
                    dve.tensor_tensor(gatew[:, :, :], top[:, :, :], den[:, :].unsqueeze(1).to_broadcast([P, TOPK, TT]),
                                      ALU.mult)
                elif stage == AT_RANK + 1:
                    dve.wait_ge(rank_p, 1)
                    o = spare(AT_RANK)
                    dve.tensor_copy(cand[:, :, :], o[:, 0:TT * E].rearrange("p (t e) -> p t e", e=E))
                    dve.tensor_scalar(cnti[:, :], o[:, TT * E:TT * E + E], float(P - 1), None, ALU.add).then_inc(rank_s, 1)
                    dve.wait_ge(rank_s, 1)
                    link(dve.tensor_scalar(cnti[:, :], cnti[:, :], P.bit_length() - 1, None, ALU.arith_shift_right))
                    link(dve.tensor_copy(cnt[:, 0], cnti[:, :]))
                    link(dve.tensor_tensor_scan(cnt[:, 1], one, cnt[:, 0], 0.0, ALU.mult, ALU.add))
                    link(dve.tensor_tensor(cnt[:, 2], cnt[:, 1], cnt[:, 0], ALU.subtract))
                    link(dve.tensor_scalar(cnt[:, 3], cnt[:, 2], float(P), None, ALU.mult))
                    link(dve.tensor_tensor(cand[:, :, :], cand[:, :, :], cnt[:, 3].unsqueeze(1).to_broadcast([P, TT, E]),
                                           ALU.add))
                elif stage == AT_RANK + 2:
                    for k in range(TOPK):
                        link(dve.tensor_tensor(oh[:, k], oh[:, k], cand[:, :, :], ALU.mult))
                    link(dve.tensor_reduce(pos[:, :], oh[:, :, :, :].rearrange("p k t e -> p (k t) e"), AX.X, ALU.add))
                    link(dve.tensor_copy(posi[:, 0], pos[:, :]))
                    link(dve.tensor_scalar(posi[:, 1], posi[:, 0], P - 1, None, ALU.bitwise_and))
                    link(dve.tensor_scalar(posi[:, 2], posi[:, 0], P.bit_length() - 1, None, ALU.arith_shift_right))
                    link(dve.tensor_copy(posf[:, :, :], posi[:, 1:3]))
                elif stage == AT_RANK + 3:
                    places_onehot(0)
                elif stage == AT_RANK + 4:
                    places_onehot(1)
                elif stage == AT_RANK + 5:
                    link(dve.tensor_tensor(tile_oh[:, :, :], tileno.unsqueeze(1).to_broadcast([P, TK, NS]),
                                           posf[:, 1].unsqueeze(2).to_broadcast([P, TK, NS]), ALU.is_equal))
                elif stage == AT_RANK + 6:
                    dve.tensor_tensor(val[:, :, 0], tile_oh[:, :, :], turn.unsqueeze(2).to_broadcast([P, TK, NS]), ALU.mult)
                    dve.tensor_scalar(val[:, :, 1], tile_oh[:, :, :], row1, None, ALU.mult).then_inc(val_s, 1)
                elif stage == AT_RANK + 7:
                    link(dve.tensor_tensor(owner[:, :, :], tileno.unsqueeze(2).to_broadcast([P, NS, E]),
                                           cnt[:, 1].unsqueeze(1).to_broadcast([P, NS, E]), ALU.is_ge))
                    link(dve.tensor_reduce(slot[:, 0], owner[:, :, :], AX.X, ALU.add))
                    link(dve.tensor_scalar(expert[:, 1:NS + 1], slot[:, 0], float(E - 1), None, ALU.min))
                elif stage == AT_SLOT + 1:
                    dve.wait_ge(slot_p, 1)
                    who = spare(AT_SLOT)[:, 0:2 * NS].rearrange("p (k s) -> p k s", k=2)
                    dve.tensor_copy(slot[:, 0:2], who).then_inc(who_s, 1)
                    dve.wait_ge(who_s, 1)
                    link(dve.scalar_tensor_tensor(slot[:, 2], slot[:, 0], float(P), slot[:, 1], ALU.mult, ALU.add))
                    link(dve.tensor_scalar(slot[:, 3], slot[:, 1], 0.0, float(NONE), ALU.is_equal, ALU.mult))
                    dve.tensor_scalar(sloti[:, 0], slot[:, 2], -1.0, 0.0, ALU.add, ALU.max)
                    link(dve.scalar_tensor_tensor(sloti[:, 1], slot[:, 2], -1.0, slot[:, 3], ALU.add, ALU.add))
                    dve.tensor_scalar(sloti[:, 0], sloti[:, 0], T - 1, None, ALU.bitwise_and).then_inc(routed, 1)
                    dve.wait_ge(routed, 1)
                    dve.tensor_copy(ixg[:, :], sloti[:, 0, 0:RING]).then_inc(ixg_s, RING)

            def hidden(n, w, boff, j):
                wait(dve, silu_s, n + 1)
                wait(dve, ht_p, n - 1)
                dve.tensor_tensor(hid[:, j % 2, 0:w], act_s[:, j % 2, 0:w], bank[j % 2][:, boff:boff + w],
                                  ALU.mult).then_inc(hid_s, 1)

            def rest(n, w, j):
                p, k = w
                wait(dve, hi_s, n + 1)
                wait(dve, lo_s, n - 1)
                dve.tensor_tensor(hres[0:p, j % 2, 0:k], HT(j)[0:p, 0:k], hT3[0:p, j % 2, 0, 0:k],
                                  ALU.subtract).then_inc(res_s, 1)

            def lo(n, w, j):
                p, k = w
                wait(dve, mid_s, n + 1)
                wait(dve, y_p, n - 1)
                dve.tensor_tensor(hT3[0:p, j % 2, 2, 0:k], hres[0:p, j % 2, 0:k], hT3[0:p, j % 2, 1, 0:k],
                                  ALU.subtract).then_inc(lo_s, 1)

            def base(t, j, b):
                wait(dve, y_p, t + 1)
                dve.tensor_tensor(yo[:, j, :], YP(j), modb[:, b, 3 * D:], ALU.mult).then_inc(y_s, 1)
                wait(dve, y_s, t + 1)
                dve.tensor_tensor(xs[:, t, :], xs[:, t, :], yo[:, j, :], ALU.add).then_inc(sh_s, 1)

            hidden(0, SI, 512, 0)
            hidden(1, SI, 512, 1)
            for t in range(TT):
                rest(t, SHARED_W, t)
                if 0 < t < TT - 1:
                    hidden(t + 1, SI, 512, t + 1)
                route(t)
                if t > 0:
                    base(t - 1, (t - 1) % 2, (t - 1) // U)
                lo(t, SHARED_W, t)
            base(TT - 1, 1, B - 1)

            def rows_turned(s, j, i):
                wait(dve, rT_p, s + 1)
                wait(dve, up_p, TT + s - 1)
                dve.tensor_copy(rT[:, j % 2].rearrange("p q t -> p (q t)"), RTP(j)).then_inc(rT_s, 1)

            def fetch_rows(s, j):
                settle(dve)
                dve.tensor_copy(ixg[:, j:j + 1], sloti[:, 0, bass.ds(s, 1)]).then_inc(ixg_s, 1)

            def give_rows(s, j, i):
                wait(dve, put[j], 16 * i)
                settle(dve)
                dve.tensor_copy(ixp[:, j:j + 1], sloti[:, 1, bass.ds(s, 1)]).then_inc(ixp_s, 1)

            def step(s, j, i):
                if not (isinstance(s, int) and s + RING >= NS):
                    fetch_rows(*later(i, j, RING)[:2])
                rest(TT + s, EXPERT_W, j)
                if not (isinstance(s, int) and s + 1 == NS):
                    hidden(TT + s + 1, I, I, j + 1)
                if not (isinstance(s, int) and s + 2 >= NS):
                    rows_turned(*later(i, j, 2))
                lo(TT + s, EXPERT_W, j)
                if not (isinstance(s, int) and s == 0):
                    give_rows(*later(i, j, -1))

            def finish(b):
                dve.wait_ge(f_c, b + 1)
                v = xs[:, U * b:U * b + U, :]
                dve.tensor_tensor(v, v, yk[:, 0, U * b:U * b + U, :], ALU.add).then_inc(f_d, 1)

            rows_turned(0, 0, 0)
            hidden(TT, I, I, 0)
            rows_turned(1, 1, 0)
            over_tiles(dve, step, NS, RING)
            give_rows(NS - 1, RING - 1, NS // RING - 1)

            for b in range(B):
                dve.wait_ge(f_a, b + 1)
                for u in range(U):
                    k = U * b + u
                    last = dve.scalar_tensor_tensor(yk[:, 0, k], yk[:, 1, k], gatew[:, 1, k:k + 1], yk[:, 0, k],
                                                    ALU.mult, ALU.add)
                last.then_inc(f_b, 1)
                if b:
                    finish(b - 1)
            finish(B - 1)

        @block.tensor
        def _(pe):
            pe.wait_ge(c_silu, 1)
            for j in range(3):
                pe.wait_ge(ld_wm[j], 16)
                o = bank[j // 2][0:B, (j % 2) * 512:(j % 2 + 1) * 512]
                for c in range(C):
                    last = pe.matmul(o, cts[:, c, :], wms[:, c, j * 512:(j + 1) * 512], start=c == 0, stop=c == C - 1)
                last.then_inc(mod_p, 1)
            pe.wait_ge(ld_w, 80)
            pe.wait_ge(mod_c, 1)
            for k in range(4):
                last = pe.transpose(M1[:, k * B:(k + 1) * B], modrow[:, k * P:(k + 1) * P], ident[0:B, 0:B])
            last.then_inc(modT_p, 1)

            def turn_x(b):
                wait(pe, ln_xn, b + 1)
                wait(pe, k_s, b)
                for c in range(C):
                    for u in range(U):
                        last = pe.transpose(M0[:, c * N + u * P:c * N + (u + 1) * P],
                                            xn[:, u, c * P:(c + 1) * P], ident)
                last.then_inc(hT_p, 1)

            def product(bank_half, off, c, done):
                for k in range(C):
                    last = pe.matmul(bank_half[:, c * N:(c + 1) * N], wqkv[:, k, off + c * P:off + (c + 1) * P],
                                     hT[:, k, WIN:WIN + N], start=k == 0, stop=k == C - 1)
                if c == C - 1:
                    last.then_inc(done, 1)

            def make_q(b, c):
                if c == 0:
                    wait(pe, hT_s, b + 1)
                    wait(pe, q_s, b)
                product(M1, 0, c, q_p)

            def make_k(b, c):
                product(M0, D, c, k_p)

            def make_v(b, u):
                wait(pe, hw_s, b + 1)
                wait(pe, z_s, NQ * U * b)
                for w in range(U * u, U * u + 2):
                    for k in range(C):
                        last = pe.matmul(ZP[:, w * D:(w + 1) * D], hw[:, k, BPT * w:BPT * (w + 1), :],
                                         wqkv[:, k, 2 * D:3 * D], start=k == 0, stop=k == C - 1)
                last.then_inc(v_p, 1)

            def scores(it, u):
                n = U * it + u
                wait(pe, q_s, it + 1)
                wait(pe, k_s, it + 1)
                wait(pe, ga_s, n - U + 1)
                for s in range(2):
                    pe.matmul(SP[u][:, s * 512:(s + 1) * 512], identb, addmask(u), start=True, stop=False,
                              skip_group_check=True)
                for c in range(C):
                    for b in range(BL):
                        for s in range(2):
                            q0 = u * P + b * QB
                            r, o = b % BPT, ((s * C + c) * 2 + b // BPT) * P
                            last = pe.matmul(SP[u][KB * r:KB * (r + 1), o:o + P],
                                             kT[GC * s:GC * (s + 1), c, q0:q0 + KB],
                                             qbd[GC * s:GC * (s + 1), c, q0:q0 + QB, :],
                                             start=False, stop=True, skip_group_check=True)
                last.then_inc(s_p, 1)

            def turn_s(it, u):
                wait(pe, s_m, U * it + u + 1)
                for j in range(NBLK // BPT):
                    last = pe.transpose(SP[u][:, j * P:(j + 1) * P], ST[:, u, j, :], ident)
                last.then_inc(st_p, 1)

            def turn_p(it, u):
                wait(pe, s_nm[u], it + 1)
                for j in range(NBLK // BPT):
                    last = pe.transpose(SP[u][:, j * P:(j + 1) * P], S[:, u, BPT * j:BPT * (j + 1), :], ident)
                last.then_inc(pt_p, 1)

            def times_v(it, k):
                u, r = divmod(k, NQ)
                if k < U:
                    wait(pe, v_s, U * it + k + 1)
                if r == 0:
                    wait(pe, pt_s, U * it + u + 1)
                wait(pe, z_s, NQ * U * it + k - 1)
                for q in range(2):
                    for c in range(C):
                        for s in range(2):
                            g, o = 2 * c + s, (r % 2) * 512 + (q * C + c) * P
                            last = pe.matmul(ZP[GC * s:GC * (s + 1), o:o + P],
                                             vw[KB * r:KB * (r + 1), 2 * u + q, g * GC:(g + 1) * GC],
                                             PT[KB * r:KB * (r + 1), u, (s * C + c) * 2 + q, :],
                                             start=True, stop=True, skip_group_check=True)
                last.then_inc(z_p, 1)

            def project(it, u):
                n = U * it + u
                wait(pe, o_s, n + 1)
                o = SP[u][:, 512:512 + D]
                pe.matmul(o, ones_row[:, :], pb[:, :], start=True, stop=False)
                for c in range(C):
                    last = pe.matmul(o, OT[:, u, c, :], wpj[:, c, :], start=False, stop=c == C - 1)
                last.then_inc(pr_p, 1)

            def turn_parts(b, units):
                wait(pe, p_lo, b + 1)
                if isinstance(b, int) and b == B - 1:
                    pe.wait_ge(lg_s, b)
                wait(pe, z_s, NQ * units)
                for u in range(U):
                    for q in range(PARTS * C):
                        last = pe.transpose(MB[u][:, q * P:(q + 1) * P],
                                            h3[:, u, q // C, (q % C) * P:(q % C + 1) * P], identb)
                last.then_inc(xT_p, 1)

            def gate(b):
                wait(pe, xT_s, b + 1)
                for u in range(U):
                    for q in range(PARTS * C):
                        last = pe.matmul(LG[u], xT[:, U * b + u, q, :], gw3[:, q % C].rearrange("p k e -> p (k e)"),
                                         start=q == 0, stop=q == PARTS * C - 1)
                last.then_inc(lg_p, 1)

            def main(it, first, after):
                if after:
                    turn_x(it + 1)
                scores(it, 1)
                if after:
                    make_q(it + 1, 0)
                    make_q(it + 1, 1)
                turn_s(it, 1)
                make_v(it, 0)
                turn_p(it, 0)
                make_v(it, 1)
                for k in range(NQ * U):
                    times_v(it, k)
                    if k == 1:
                        turn_p(it, 1)
                    if k == 3 and after:
                        make_k(it + 1, 0)
                    if k == 5 and after:
                        make_k(it + 1, 1)
                    if k == 6:
                        project(it, 0)
                if after:
                    scores(it + 1, 0)
                if not first:
                    turn_parts(it - 1, U * (it + 1))
                project(it, 1)
                if after:
                    turn_s(it + 1, 0)
                if not first:
                    gate(it - 1)

            turn_x(0)
            for c in range(C):
                make_q(0, c)
            for c in range(C):
                make_k(0, c)
            scores(0, 0)
            turn_s(0, 0)
            over(pe, main)

            def turn_hidden(n, k, p, j):
                wait(pe, hid_s, n + 1)
                wait(pe, res_s, n - 1)
                for q in range(k):
                    last = pe.transpose(HT(j)[0:p, q, :], hid[:, j % 2, q * p:(q + 1) * p], ident)
                last.then_inc(ht_p, 1)

            def up_shared(t, j):
                wait(pe, hid_s, t - 1)
                for half in range(2):
                    for q in range(PARTS * C):
                        last = pe.matmul(bank[j % 2][:, half * 512:half * 512 + SI], xT[:, t, q, :],
                                         sw13[:, q % C, half * SI:(half + 1) * SI],
                                         start=q == 0, stop=q == PARTS * C - 1)
                last.then_inc(up_p, 1)

            def down_shared(t, j):
                wait(pe, lo_s, t + 1)
                wait(pe, y_s, t - 1)
                if t == AT_RANK:
                    pe.wait_ge(rank_s, 1)
                if t == AT_SLOT:
                    pe.wait_ge(who_s, 1)
                last_k = SI - (SK - 1) * P
                for k in range(SK):
                    p = P if k < SK - 1 else last_k
                    for q in range(PARTS):
                        last = pe.matmul(YP(j), hT3[0:p, j % 2, q, k, :], sw2[0:p, k, :],
                                         start=k == 0 and q == 0, stop=k == SK - 1 and q == PARTS - 1)
                last.then_inc(y_p, 1)

            def places(o):
                pe.wait_ge(ohb_s, 1)
                pe.matmul(o[:, 0:(TT + 1) * E], before, ohb[:, :, :].rearrange("p t e -> p (t e)"), start=True, stop=False,
                          skip_group_check=True)
                for t in range(TT):
                    last = pe.matmul(o[:, (t + 1) * E:(TT + 1) * E].rearrange("p (t e) -> p t e", e=E), onesb,
                                     ohb[:, t, :].unsqueeze(1).to_broadcast([P, TT - t, E]), start=False, stop=t == TT - 1,
                                     skip_group_check=True)
                last.then_inc(rank_p, 1)

            def sitters(o):
                pe.wait_ge(val_s, 1)
                for k in range(TOPK * TT):
                    last = pe.matmul(o[:, 0:2 * NS], lane_oh[:, k, :], val[:, k].rearrange("p v s -> p (v s)"),
                                     start=k == 0, stop=k == TOPK * TT - 1)
                last.then_inc(slot_p, 1)

            pe.wait_ge(ld_sw, 32)
            pe.wait_ge(ga_s, TT)
            up_shared(0, 0)
            up_shared(1, 1)
            turn_parts(B - 1, U * B)
            gate(B - 1)
            pe.wait_ge(lg_s, B)
            for t in range(TT):
                turn_hidden(t, SK, P, t)
                if 0 < t < TT - 1:
                    up_shared(t + 1, t + 1)
                if t > 0:
                    down_shared(t - 1, t - 1)
                if t in (AT_RANK, AT_SLOT):
                    pe.wait_ge(y_s, t - 1)
                    (places if t == AT_RANK else sitters)(spare(t))
            down_shared(TT - 1, 1)

            def turn_rows(s, j, i):
                wait(pe, fetch[j], 16 * (i + 1))
                wait(pe, rT_s, s - 1)
                if isinstance(s, int) and s < 2:
                    pe.wait_ge(hid_s, TT)
                for q in range(PARTS * C):
                    last = pe.transpose(RTP(j)[:, q * P:(q + 1) * P], rows[:, j, q * P:(q + 1) * P], identb)
                last.then_inc(rT_p, 1)

            held = [pe.alloc_register(f"expert_of_tile{k}") for k in range(RING + 2)]
            experts = [None] * (RING + 2)

            def load_experts(i):
                if isinstance(i, int) and i == 0:
                    pe.reg_load(held[1:], expert[0:1, 1:RING + 2])
                else:
                    pe.reg_mov(held[0], held[RING])
                    pe.reg_mov(held[1], held[RING + 1])
                    pe.reg_load(held[2:], expert[0:1, bass.ds(RING * i + 2, RING)])
                experts[:] = [pe.snap(r, min_val=0, max_val=E - 1) for r in held[1 if isinstance(i, int) and i == 0 else 0:]]
                if len(experts) == RING + 1:
                    experts.insert(0, None)

            def up(s, j, e):
                wait(pe, rT_s, s + 1)
                wait(pe, hid_s, TT + s - 1)
                for q in range(PARTS * C):
                    last = pe.matmul(bank[j % 2][:, 0:2 * I], rT[:, j % 2, q, :], w13[:, q % C, bass.ds(e, 1), :],
                                     start=q == 0, stop=q == PARTS * C - 1)
                last.then_inc(up_p, 1)

            def down(s, j, e):
                wait(pe, lo_s, TT + s + 1)
                if isinstance(s, int) and s < 2:
                    pe.wait_ge(y_s, TT + s - 1)
                else:
                    wait(pe, yo_s, s - 1)
                for k in range(2):
                    for q in range(PARTS):
                        last = pe.matmul(YP(j), hT3[0:IH, j % 2, q, k, :], w2[:, k, bass.ds(e, 1), :],
                                         start=k == 0 and q == 0, stop=k == 1 and q == PARTS - 1)
                last.then_inc(y_p, 1)

            def step(s, j, i):
                if j == 0 and not (isinstance(s, int) and s == 0):
                    load_experts(i)
                turn_hidden(TT + s, 2, IH, j)
                if not (isinstance(s, int) and s + 1 == NS):
                    up(s + 1, j + 1, experts[j + 2])
                if not (isinstance(s, int) and s + 2 >= NS):
                    turn_rows(*later(i, j, 2))
                if not (isinstance(s, int) and s == 0):
                    down(s - 1, j + 1, experts[j])

            pe.wait_ge(ld_ew, 32)
            pe.wait_ge(routed, 1)
            turn_rows(0, 0, 0)
            load_experts(0)
            up(0, 0, experts[1])
            turn_rows(1, 1, 0)
            over_tiles(pe, step, NS, RING)
            down(NS - 1, NS - 1, experts[RING])


_OUT = (B, N, D)


def kernel(**inputs):
    import numpy as np
    import ml_dtypes
    import concourse.bacc as bacc
    from concourse.bass_utils import run_bass_kernel_spmd as run

    a = {k: np.asarray(v) for k, v in inputs.items()}

    row = np.arange(P)
    t, h = row // GH, row % GH
    j = np.arange(KB)
    d = j[None, :] - WIN - t[:, None]
    inside = (d >= -WIN) & (d < WIN)
    m = np.where(inside, (WIN - np.abs(d) / 2.0) / WIN * HD ** -0.5, 1.0)
    cf = np.zeros((P, FCW), np.float32)
    cf[:, slice(*FC["ident"])] = np.eye(P)
    cf[:, slice(*FC["window"])] = np.tile(m.T, (BPT, 1))
    cf[:, slice(*FC["headsel"])] = ((row % GC) // HD)[:, None] == np.arange(GH)[None, :]
    cf[:, slice(*FC["nhalf"])] = -0.5
    cf[:, slice(*FC["rev"])] = E - np.arange(E)
    cf[:, slice(*FC["lane"])] = row
    cf[:, slice(*FC["tile"])] = np.arange(NS)
    cf[:, slice(*FC["turn"])] = np.arange(TOPK * TT)
    cf[:, slice(*FC["row1"])] = row[:, None] + 1
    cf[:, slice(*FC["one"])] = 1.0
    cb = np.zeros((P, BCW), np.float32)
    cb[:, 0:P] = np.eye(P)
    cb[:, BCW - 2 * P:BCW - P] = row[:, None] < row[None, :]
    cb[:, BCW - P:] = 1.0
    for u in range(U):
        key = u * P + QB * np.arange(BL)[:, None] + j[None, :] - WIN
        ok = inside.T[None, :, :] & ((key >= 0) & (key < N))[:, :, None]
        ok = ok.reshape(2, P, P).transpose(1, 0, 2)
        ok = np.broadcast_to(ok[:, None], (P, C, 2, P))
        cb[:, P + u * 4 * P:P + (u + 1) * 4 * P] = np.where(ok, 0.0, -1e30).reshape(P, -1)
    cb = cb.astype(ml_dtypes.bfloat16)

    w13 = np.concatenate([a["L0_ffn_w1"], a["L0_ffn_w3"]], axis=1)
    sw13 = np.concatenate([a["L0_ffn_sw1"], a["L0_ffn_sw3"]], axis=0)
    sw2 = np.zeros((SK * P, D), a["L0_ffn_sw2"].dtype)
    sw2[:SI] = a["L0_ffn_sw2"].T
    arrays = {
        "gateT": a["L0_ffn_gate_w"].T,
        "w13T": w13.reshape(E, 2 * I, C, P).transpose(3, 2, 0, 1),
        "w2T": a["L0_ffn_w2"].reshape(E, D, 2, IH).transpose(3, 2, 0, 1),
        "sw13T": sw13.reshape(2 * SI, C, P).transpose(2, 1, 0),
        "sw2T": sw2.reshape(SK, P, D).transpose(1, 0, 2),
        "x": a["L0_attn_x"].reshape(T, D),
        "wqkvT": a["L0_attn_qkv_w"].T,
        "projT": a["L0_attn_proj_w"].T,
        "proj_b": a["L0_attn_proj_b"].reshape(1, D),
        "cT": a["L0_c"].T,
        "wmod": a["L0_wmod"],
        "cf": cf,
        "cb": cb,
    }
    arrays = {k: np.ascontiguousarray(v) for k, v in arrays.items()}
    nc = bacc.Bacc("TRN2", target_bir_lowering=False, num_devices=1)
    args = {k: nc.dram_tensor(k, v.shape, mybir.dt.from_np(v.dtype), kind="ExternalInput").ap()
            for k, v in arrays.items()}
    out = nc.dram_tensor("out", (T, D), F32, kind="ExternalOutput").ap()
    build(nc, **args, out=out)
    r = run(nc, [arrays], core_ids=[0])
    return r.results[0]["out"].reshape(_OUT)
```
